# Optimizing a Trainium2 kernel written in Bass

```python
import numpy as np
import jax
import jax.numpy as jnp

def _softmax(x, axis=-1):
    return jax.nn.softmax(x, axis=axis)

def _gelu(x):
    return jax.nn.gelu(x, approximate=True)

def _silu(x):
    return jax.nn.silu(x)

def _sigmoid(x):
    return jax.nn.sigmoid(x)

def _layernorm(x, axis=-1, eps=1e-05):
    m = jnp.mean(x, axis=axis, keepdims=True)
    v = jnp.var(x, axis=axis, keepdims=True)
    return (x - m) / jnp.sqrt(v + eps)

def _scatter_add(tgt, idx, src, axis=0):
    return tgt.at[idx].add(src)

def _segment_sum(src, seg, n):
    return jax.ops.segment_sum(src, seg, n)
kernel_name = 'mk_adaln_d1_jaxref_r8_ce9057'

def setup_inputs(seed: int=0):
    np.random.seed(seed)
    _w = jnp.asarray

    def _L0_attn_setup():
        import jax, jax.numpy as jnp
        import numpy as np
        BATCH, SEQ, D_MODEL, D_STATE = (8, 512, 128, 16)
        LN_EPS = 1e-05
        key = jax.random.key(seed)
        ks = jax.random.split(key, 8)
        lin = lambda k, i, o: jax.random.normal(k, (i, o), jnp.float32) * (1.0 / np.sqrt(i))
        return {'x': jax.random.normal(ks[0], (BATCH, SEQ, D_MODEL), jnp.float32), 'ln_gamma': jnp.ones((D_MODEL,), jnp.float32), 'ln_beta': jnp.zeros((D_MODEL,), jnp.float32), 'A': jax.random.normal(ks[1], (D_STATE, D_STATE), jnp.float32) * 0.01, 'C': jax.random.normal(ks[2], (D_STATE, D_MODEL), jnp.float32) * 0.01, 'w_delta': lin(ks[3], D_MODEL, D_STATE), 'b_delta': jnp.zeros((D_STATE,), jnp.float32), 'w_in': lin(ks[4], D_MODEL, D_STATE), 'b_in': jnp.zeros((D_STATE,), jnp.float32), 'w_gate': lin(ks[5], D_MODEL, D_MODEL), 'b_gate': jnp.zeros((D_MODEL,), jnp.float32)}
    _L0_attn_in = _L0_attn_setup()

    def _L0_ffn_setup():
        import jax, jax.numpy as jnp
        import numpy as np
        B, S, H = (2, 256, 128)
        I = 64
        E_R, E_Z = (32, 8)
        E_T = E_R + E_Z
        K = 6
        SCALE = 2.5
        W_INIT = 0.02
        key = jax.random.key(seed)
        k0, k1, k2, k3 = jax.random.split(key, 4)
        return {'hidden_states': jax.random.normal(k0, (B, S, H), jnp.float32), 'classifier_weight': jax.random.normal(k1, (E_T, H), jnp.float32) * W_INIT, 'e_score_correction_bias': jnp.zeros((E_T,), jnp.float32), 'gate_up_proj': jax.random.normal(k2, (E_T, 2 * I, H), jnp.float32) * W_INIT, 'down_proj': jax.random.normal(k3, (E_R, H, I), jnp.float32) * W_INIT}
    _L0_ffn_in = _L0_ffn_setup()
    _L0_c = _w((lambda *s: np.random.randn(*s).astype(np.float32) * 0.05)(8, 128))
    _L0_wmod = _w((lambda *s: np.random.randn(*s).astype(np.float32) * 0.05)(128, 6 * 128) * 128 ** (-0.5))
    _d = {'L0_attn_x': _L0_attn_in['x'], 'L0_attn_ln_gamma': _L0_attn_in['ln_gamma'], 'L0_attn_ln_beta': _L0_attn_in['ln_beta'], 'L0_attn_A': _L0_attn_in['A'], 'L0_attn_C': _L0_attn_in['C'], 'L0_attn_w_delta': _L0_attn_in['w_delta'], 'L0_attn_b_delta': _L0_attn_in['b_delta'], 'L0_attn_w_in': _L0_attn_in['w_in'], 'L0_attn_b_in': _L0_attn_in['b_in'], 'L0_attn_w_gate': _L0_attn_in['w_gate'], 'L0_attn_b_gate': _L0_attn_in['b_gate'], 'L0_ffn_classifier_weight': _L0_ffn_in['classifier_weight'], 'L0_ffn_e_score_correction_bias': _L0_ffn_in['e_score_correction_bias'], 'L0_ffn_gate_up_proj': _L0_ffn_in['gate_up_proj'], 'L0_ffn_down_proj': _L0_ffn_in['down_proj'], 'L0_c': _L0_c, 'L0_wmod': _L0_wmod}
    _x0 = _d['L0_attn_x']
    _d['L0_attn_x'] = jax.random.normal(jax.random.fold_in(jax.random.key(seed), 1), (8, 512, 128), dtype=_x0.dtype)
    del _x0
    return _d

def reference(L0_attn_x, L0_attn_ln_gamma, L0_attn_ln_beta, L0_attn_A, L0_attn_C, L0_attn_w_delta, L0_attn_b_delta, L0_attn_w_in, L0_attn_b_in, L0_attn_w_gate, L0_attn_b_gate, L0_ffn_classifier_weight, L0_ffn_e_score_correction_bias, L0_ffn_gate_up_proj, L0_ffn_down_proj, L0_c, L0_wmod):

    def _L0_attn_ref(x, ln_gamma, ln_beta, A, C, w_delta, b_delta, w_in, b_in, w_gate, b_gate):
        import jax, jax.numpy as jnp
        import numpy as np
        BATCH, SEQ, D_MODEL, D_STATE = (8, 512, 128, 16)
        LN_EPS = 1e-05
        mu = jnp.mean(x, axis=-1, keepdims=True)
        var = jnp.var(x, axis=-1, keepdims=True)
        xn = (x - mu) / jnp.sqrt(var + LN_EPS) * ln_gamma + ln_beta
        delta = jax.nn.sigmoid(jnp.einsum('btd,ds->bts', xn, w_delta) + b_delta)
        B_t = jnp.einsum('btd,ds->bts', xn, w_in) + b_in
        gate = jax.nn.sigmoid(jnp.einsum('btd,de->bte', xn, w_gate) + b_gate)

        def step(h, inp):
            d_t, b_t = inp
            h_new = jnp.tanh(h * d_t @ A + b_t)
            return (h_new, h_new)
        h0 = jnp.zeros((x.shape[0], A.shape[0]), x.dtype)
        _, hs = jax.lax.scan(step, h0, (jnp.swapaxes(delta, 0, 1), jnp.swapaxes(B_t, 0, 1)))
        y = jnp.swapaxes(jnp.einsum('tbs,se->tbe', hs, C), 0, 1) * gate
        return y + x

    def _L0_ffn_ref(hidden_states, classifier_weight, e_score_correction_bias, gate_up_proj, down_proj):
        import jax, jax.numpy as jnp
        import numpy as np
        B, S, H = (2, 256, 128)
        I = 64
        E_R, E_Z = (32, 8)
        E_T = E_R + E_Z
        K = 6
        SCALE = 2.5
        W_INIT = 0.02
        orig_shape = hidden_states.shape
        x = hidden_states.reshape(-1, H).astype(jnp.float32)
        T = x.shape[0]
        logits = x @ classifier_weight.T
        scores = jax.nn.softmax(logits, axis=-1)
        _, topk_idx = jax.lax.top_k(scores + e_score_correction_bias[None, :], K)
        topk_w = jnp.take_along_axis(scores, topk_idx, axis=1) * SCALE
        w_full = jnp.zeros((T, E_T), jnp.float32).at[jnp.arange(T)[:, None], topk_idx].add(topk_w)
        zero_w = w_full[:, E_R:].sum(axis=-1, keepdims=True)
        out0 = x * zero_w
        routed_w = w_full[:, :E_R].T

        def body(out, xs):
            Wgu, Wd, we = xs
            gate, up = jnp.split(x @ Wgu.T, 2, axis=-1)
            y = jax.nn.silu(gate) * up @ Wd.T
            return (out + we[:, None] * y, None)
        out, _ = jax.lax.scan(body, out0, (gate_up_proj[:E_R], down_proj, routed_w))
        return out.reshape(orig_shape).astype(hidden_states.dtype)
    x = L0_attn_x
    mod = (_silu(L0_c) @ L0_wmod).reshape(L0_c.shape[0], 6, 1, -1)
    sa, ca, ga, sb, cb, gb = (mod[:, 0], mod[:, 1], mod[:, 2], mod[:, 3], mod[:, 4], mod[:, 5])
    ga = (2 * (ga >= 0) - 1) * jnp.maximum(jnp.abs(ga), 0.25)
    gb = (2 * (gb >= 0) - 1) * jnp.maximum(jnp.abs(gb), 0.25)
    h = _layernorm(x, axis=-1) * (1 + ca) + sa
    x = x + ga * _L0_attn_ref(h, L0_attn_ln_gamma, L0_attn_ln_beta, L0_attn_A, L0_attn_C, L0_attn_w_delta, L0_attn_b_delta, L0_attn_w_in, L0_attn_b_in, L0_attn_w_gate, L0_attn_b_gate)
    h = _layernorm(x, axis=-1) * (1 + cb) + sb
    x = x + gb * _L0_ffn_ref(h, L0_ffn_classifier_weight, L0_ffn_e_score_correction_bias, L0_ffn_gate_up_proj, L0_ffn_down_proj)
    return x

_drawn_inputs = setup_inputs


def setup_inputs(seed=0):
    import zlib

    import numpy as np

    out = dict(_drawn_inputs(seed))
    spreads = {'L0_attn_ln_gamma': (1.0, 0.6),
     'L0_attn_ln_beta': (0.0, 0.8),
     'L0_attn_b_delta': (0.0, 2.0),
     'L0_attn_b_in': (0.0, 2.0),
     'L0_attn_b_gate': (0.0, 2.0),
     'L0_ffn_e_score_correction_bias': (0.0, 0.394)}
    factors = {'L0_attn_A': 77.659,
     'L0_attn_C': 8.0,
     'L0_attn_w_delta': 82.413,
     'L0_attn_w_in': 8.0,
     'L0_attn_w_gate': 8.0,
     'L0_ffn_classifier_weight': 7.422,
     'L0_ffn_gate_up_proj': 8.0,
     'L0_ffn_down_proj': 8.0}
    for name, (base, spread) in spreads.items():
        noise = np.random.default_rng([zlib.crc32(name.encode()), seed]).standard_normal(out[name].shape)
        drawn = base * np.exp(spread * noise) if base else spread * noise
        out[name] = jnp.asarray(drawn.astype(out[name].dtype))
    for name, factor in factors.items():
        out[name] = (out[name] * factor).astype(out[name].dtype)
    return out
```

```python
from contextlib import ExitStack

import concourse.bass as bass
from concourse import mybir

F32 = mybir.dt.float32
F32R = mybir.dt.float32r
BF16 = mybir.dt.bfloat16
I32 = mybir.dt.int32
U32 = mybir.dt.uint32
ALU = mybir.AluOpType
ACT = mybir.ActivationFunctionType
AX = mybir.AxisListType.X

P = 128
EPS = 1e-5
TOP_K = 6
ROUTE_SCALE = 2.5
MOD_FLOOR = 0.25


def adaln_block(nc, x, ln_gamma, ln_beta, A, C, w_delta, b_delta, w_in, b_in, w_gate, b_gate,
                classifier, route_bias, gate_up, down, cond, wmod, out):
    B, T, D = x.shape
    S = A.shape[0]
    NT = T // P
    SEG_LEN = 16
    SEGS = T // SEG_LEN
    E_T = classifier.shape[0]
    E_R = down.shape[0]
    INNER = down.shape[2]
    PAIRS = E_R // 2
    NMOD = wmod.shape[1] // D
    assert D == P and B * S == P and 2 * INNER == P and NT * P == 512 and gate_up.shape[1] == 2 * INNER

    with ExitStack() as ctx:
        def sb(name, shape, dt=F32):
            return ctx.enter_context(nc.sbuf_tensor(name, shape, dt))

        def sem(name):
            return ctx.enter_context(nc.semaphore(name))

        bank = ctx.enter_context(nc.psum_tensor("bank", [P, 8, 512], F32))
        SCAN = (0, 1)
        SIDE = (2, 3, 4, 5)
        GATE_B, UP_B = (0, 1), (2, 3)
        ROUTE_B, DOWN_B = 4, 5
        MISC = (6, 7)
        DELTA_B, DRIVE_B = 0, 1
        SETUP_B = 2

        ident = sb("ident", [P, P])
        ident_bf = sb("ident_bf", [P, P], BF16)
        ones_row = sb("ones_row", [1, P])
        own_batch = sb("own_batch", [P, B])
        every_batch = sb("every_batch", [S, B, S])
        minus_half = sb("minus_half", [P, NT])
        expert_no = sb("expert_no", [P, E_T])
        pick_pair = sb("pick_pair", [96, PAIRS, P], BF16)

        c_row = sb("c_row", [B, P])
        c_silu = sb("c_silu", [B, P])
        c_silu_t = sb("c_silu_t", [P, B])
        wmod_sb = sb("wmod_sb", [P, NMOD * P])
        SA, CA1, GA, SB_, CB1, GB, GCB, GSB = range(8)
        modt = sb("modt", [P, 8, B])
        mod_tmp = sb("mod_tmp", [P, 2, B])
        R_SA, R_CA1, R_GA, R_GCB, R_GSB = range(5)
        rows = sb("rows", [P, 5, B, P])

        small = sb("small", [S, S + P + 2])
        small_rep = sb("small_rep", [P, S + P + 2])
        a_block = sb("a_block", [P, B, S])
        c_ga = sb("c_ga", [P, P])
        ga_rep = sb("ga_rep", [P, B, S])
        ga_t = sb("ga_t", [P, P])
        c_batch = sb("c_batch", [P, B, P])
        PAD = P - S
        wd_pad = sb("wd_pad", [P, 2 * P - S])
        wi_pad = sb("wi_pad", [P, 2 * P - S])
        w_small = sb("w_small", [P, 2, S])
        gb_col = sb("gb_col", [P, 2])
        wg_sb = sb("wg_sb", [P, P])
        bg_row = sb("bg_row", [1, P])
        cls_sb = sb("cls_sb", [E_T, P])
        cls_t = sb("cls_t", [P, E_T])
        route_bias_sb = sb("route_bias_sb", [P, E_T])

        x_all = sb("x_all", [P, B, NT, P])
        h_all = sb("h_all", [P, B, NT, P])
        xn_all = sb("xn_all", [P, B, 512])
        stats = sb("stats", [P, NT, 6])
        mom = sb("mom", [P, 5, NT])
        ve1 = sb("ve1", [P, B, NT])
        ve2 = sb("ve2", [P, B, NT])
        nm1 = sb("nm1", [P, B, NT])
        nm2 = sb("nm2", [P, B, NT])
        rs1 = sb("rs1", [P, B, NT])
        rs2 = sb("rs2", [P, B, NT])
        mr1 = sb("mr1", [P, B, NT])
        mr2 = sb("mr2", [P, B, NT])

        delta = sb("delta", [P, T])
        drive = sb("drive", [P, T])
        H = sb("H", [P, T])
        h_in = sb("h_in", [P, SEGS])
        h_in0 = sb("h_in0", [P, SEGS])
        ends = sb("ends", [P, SEGS])
        differ = sb("differ", [P, SEGS])
        differ_p = sb("differ_p", [P, 1])
        ones_col = sb("ones_col", [P, 1])
        again = sb("again", [1, 1], I32)

        gu_raw = sb("gu_raw", [P, 2, PAIRS, P])
        dn_raw = sb("dn_raw", [P, E_R, INNER])
        w_hi = sb("w_hi", [P, 3, PAIRS, P], F32R)
        w_lo = sb("w_lo", [P, 3, PAIRS, P], F32R)

        x1, z, u = x_all[:, 0, :, :], x_all[:, 1, :, :], x_all[:, 2, :, :]
        h2t = x_all[:, 3, :, :].rearrange("p j d -> p (j d)")
        raw_g = gu_raw[:, 0, :, :].rearrange("p k d -> p (k d)")
        raw_u = gu_raw[:, 1, :, :].rearrange("p k d -> p (k d)")
        raw_d = dn_raw[:, :, :].rearrange("p e i -> p (e i)")
        act4 = raw_g.rearrange("p (k n) -> p k n", k=4)
        silu_g = raw_u[:, 0:1024].rearrange("p (k n) -> p k n", k=2)
        f_t = raw_u[:, 1024:1536]
        base = raw_d[:, 0:1024].rearrange("p (k j d) -> p k j d", k=2, j=NT)
        out_sb = raw_d[:, 1024:1536].rearrange("p (j d) -> p j d", j=NT)
        v_t = raw_d[:, 1536:2048].rearrange("p (j d) -> p j d", j=NT)
        now_mod = sb("now_mod", [P, 2])
        now_gb = sb("now_gb", [P, 1])
        mean3 = sb("mean3", [P, NT])
        ve3 = sb("ve3", [P, NT])
        rs3 = sb("rs3", [P, NT])
        h2_hi = sb("h2_hi", [P, 2, 512], F32R)
        h2_lo = sb("h2_lo", [P, 2, 512], F32R)
        lmax = sb("lmax", [P, NT])
        ls = sb("ls", [P, NT, E_T])
        ex = sb("ex", [P, NT, E_T])
        esum = sb("esum", [P, NT])
        erec = sb("erec", [P, NT])
        score = sb("score", [P, NT, E_T])
        scaled = sb("scaled", [P, NT, E_T])
        biased = sb("biased", [P, NT, E_T])
        top8 = sb("top8", [P, NT, 8])
        top8_at = sb("top8_at", [P, NT, 8], U32)
        last_at = sb("last_at", [P, NT])
        above = sb("above", [P, NT, E_T])
        at_or_above = sb("at_or_above", [P, NT, E_T])
        early = sb("early", [P, NT, E_T])
        weight = sb("weight", [P, NT, E_T])
        zero_w = sb("zero_w", [P, NT])
        rest1 = sb("rest1", [P, NT, E_R])
        w3 = sb("w3", [P, NT, 3, E_R], BF16)
        w3t = sb("w3t", [96, 512], BF16)
        act_hi = sb("act_hi", [P, 4, 512], F32R)
        gated = sb("gated", [P, 2, 512])
        act_lo = sb("act_lo", [P, 4, 512], F32R)

        in_cond = sem("in_cond")
        in_wmod = sem("in_wmod")
        in_small = sem("in_small")
        in_x = [sem("in_x0"), sem("in_x1")]
        in_gu = sem("in_gu")
        in_dn = sem("in_dn")
        pool_const = sem("pool_const")
        c_silu_done = sem("c_silu_done")
        setup_mm = sem("setup_mm")
        setup_dve = sem("setup_dve")
        rows_mm = sem("rows_mm")
        rows_out = sem("rows_out")
        dve_chain = sem("dve_chain")
        stats1_done = sem("stats1_done")
        pow1_done = sem("pow1_done")
        rstd1_done = sem("rstd1_done")
        z1_done = sem("z1_done")
        scaled_done = sem("scaled_done")
        h_done = sem("h_done")
        mom1_chain = sem("mom1_chain")
        mom2_chain = sem("mom2_chain")
        mom3_chain = sem("mom3_chain")
        stats2_done = sem("stats2_done")
        pow2_done = sem("pow2_done")
        rstd2_done = sem("rstd2_done")
        z2_done = sem("z2_done")
        z2t_done = sem("z2t_done")
        xnt_done = sem("xnt_done")
        proj_done = sem("proj_done")
        proj_out = sem("proj_out")
        step_mm = sem("step_mm")
        step_h = sem("step_h")
        step_in = sem("step_in")
        verdict_mm = sem("verdict_mm")
        verdict = sem("verdict")
        more_mm = sem("more_mm")
        more_h = sem("more_h")
        more_in = sem("more_in")
        side_mm = sem("side_mm")
        side_hi = sem("side_hi")
        side_out = sem("side_out")
        res_chain = sem("res_chain")
        res_done = sem("res_done")

        gate_mm = sem("gate_mm")
        up_mm = sem("up_mm")
        route_mm = sem("route_mm")
        down_mm = sem("down_mm")
        silu_done = sem("silu_done")
        gated_done = sem("gated_done")
        act_done = sem("act_done")
        hi_done = sem("hi_done")
        lo_done = sem("lo_done")
        y_mm = sem("y_mm")
        zt_mm = sem("zt_mm")
        logit_mm = sem("logit_mm")
        w3t_mm = sem("w3t_mm")
        ft_mm = sem("ft_mm")
        pre_chain = sem("pre_chain")
        var3_done = sem("var3_done")
        rstd3_done = sem("rstd3_done")
        z_done = sem("z_done")
        u_chain = sem("u_chain")
        u_done = sem("u_done")
        h2t_done = sem("h2t_done")
        h2_hi_done = sem("h2_hi_done")
        h2_lo_done = sem("h2_lo_done")
        shifted_done = sem("shifted_done")
        exp_done = sem("exp_done")
        w3_done = sem("w3_done")
        w3t_done = sem("w3t_done")
        base_done = sem("base_done")
        f_done = sem("f_done")
        gb_ready = sem("gb_ready")
        out_ready = sem("out_ready")
        out_dma = sem("out_dma")

        x_tiles = x.rearrange("b (j p) d -> b p j d", p=P)
        out_tiles = out.rearrange("b (j p) d -> b p j d", p=P)
        gu_view = gate_up[0:E_R].rearrange("(pair e2) (gu i) h -> e2 gu i pair h", e2=2, gu=2)
        N_POOL_CONST = 14

        def wait(eng, s, value):
            if isinstance(value, int) and value <= 0:
                return
            eng.wait_ge(s, value)

        def wait_apart(eng, s, value):
            eng.wait_ge(in_small, 16 * 12)
            eng.wait_ge(s, value)

        def row(k, b):
            return rows[:, k, b, :].unsqueeze(1).broadcast_to([P, NT, P])

        SIDE_WORK = ([("rows", 0), ("rows", 1)] + [("weights", g) for g in range(3 * PAIRS // 4)]
                     + [("gate", b) for b in range(B)] + [("rows", g) for g in range(2, 6)])
        ROW_LIST = [(R_GA, GA, b) for b in range(B)] + [(R_GCB, GCB, b) for b in range(B)] \
            + [(R_GSB, GSB, b) for b in range(B)]
        SWEEP_STEPS = 2 * SEG_LEN

        block = ctx.enter_context(nc.Block())

        @block.sync
        def _(sp):
            sp.dma_start(c_row[:, :], cond).then_inc(in_cond, 16)
            sp.dma_start(wmod_sb[:, :], wmod).then_inc(in_wmod, 16)
            for b in range(B):
                sp.dma_start(x_all[:, b, :, :], x_tiles[b]).then_inc(in_x[b // (B // 2)], 16)
            for e2 in range(2):
                for gu in range(2):
                    sp.dma_start(gu_raw[e2 * INNER:(e2 + 1) * INNER, gu, :, :], gu_view[e2, gu]).then_inc(in_gu, 16)
            sp.dma_start(dn_raw[:, :, :], down.rearrange("e h i -> h e i")).then_inc(in_dn, 16)
            with sp.Fori(0, B) as b:
                sp.wait_ge(out_ready, b + 1)
                sp.dma_start(out_tiles[bass.ds(b, 1)].rearrange("a p j d -> p (a j) d"), out_sb[:, :, :]).then_inc(out_dma, 16)
            sp.wait_ge(out_dma, 16 * B)

        @block.gpsimd
        def _(pool):
            g = nc.gpsimd
            g.memset(ident[:, :], 0.0).then_inc(pool_const, 1)
            pool.wait_ge(pool_const, 1)
            g.affine_select(out=ident[:, :], in_=ident[:, :], compare_op=ALU.not_equal, fill=1.0, base=0,
                            pattern=[[-1, P]], channel_multiplier=1).then_inc(pool_const, 1)
            g.memset(minus_half[:, :], -0.5).then_inc(pool_const, 1)
            g.memset(ones_row[:, :], 1.0).then_inc(pool_const, 1)
            g.memset(own_batch[:, :], 1.0).then_inc(pool_const, 1)
            pool.wait_ge(pool_const, 5)
            g.affine_select(out=own_batch[:, :], in_=own_batch[:, :], compare_op=ALU.is_ge, fill=0.0, base=0,
                            pattern=[[-S, B]], channel_multiplier=1).then_inc(pool_const, 1)
            pool.wait_ge(pool_const, 6)
            g.affine_select(out=own_batch[:, :], in_=own_batch[:, :], compare_op=ALU.is_ge, fill=0.0, base=S - 1,
                            pattern=[[S, B]], channel_multiplier=-1).then_inc(pool_const, 1)
            g.iota(expert_no[:, :], pattern=[[1, E_T]], base=0, channel_multiplier=0,
                   allow_small_or_imprecise_dtypes=True).then_inc(pool_const, 1)
            g.memset(pick_pair[:, :, :], 0.0).then_inc(pool_const, 1)
            g.tensor_copy(every_batch[:, :, :], ident[0:S, 0:S].unsqueeze(1).broadcast_to([S, B, S])).then_inc(pool_const, 1)
            g.tensor_copy(ident_bf[:, :], ident[:, :]).then_inc(pool_const, 1)

            with pool.Fori(0, B) as b:
                pool.wait_ge(stats1_done, b + 1)
                g.tensor_tensor(rs1[:, b, :], ve1[:, b, :], minus_half[:, :], ALU.pow).then_inc(pow1_done, 1)
                pool.wait_ge(pow1_done, b + 1)
                g.tensor_tensor(mr1[:, b, :], nm1[:, b, :], rs1[:, b, :], ALU.mult).then_inc(rstd1_done, 1)
            pool.wait_ge(rows_out, 4)
            with pool.Fori(0, B) as b:
                pool.wait_ge(z1_done, b + 1)
                g.tensor_tensor(h_all[:, b, :, :], h_all[:, b, :, :], row(R_CA1, b), ALU.mult).then_inc(scaled_done, 1)
            with pool.Fori(0, B) as b:
                pool.wait_ge(stats2_done, b + 1)
                g.tensor_tensor(rs2[:, b, :], ve2[:, b, :], minus_half[:, :], ALU.pow).then_inc(pow2_done, 1)
                pool.wait_ge(pow2_done, b + 1)
                g.tensor_tensor(mr2[:, b, :], nm2[:, b, :], rs2[:, b, :], ALU.mult).then_inc(rstd2_done, 1)
            pool.wait_ge(rstd2_done, B)
            for part in range(3):
                pool.wait_ge(pool_const, 11 + part)
                at = pick_pair[E_R * part:E_R * (part + 1), :, :].rearrange("e pair (e2 i) -> e pair e2 i", e2=2)
                g.affine_select(out=at, in_=at, compare_op=ALU.not_equal, fill=1.0, base=0,
                                pattern=[[-2, PAIRS], [-1, 2], [0, INNER]], channel_multiplier=1).then_inc(pool_const, 1)
            pool.wait_ge(pool_const, N_POOL_CONST)
            pool.wait_ge(side_out, 2)
            with pool.Fori(0, B) as b:
                pool.wait_ge(z2_done, b + 1)
                g.tensor_tensor(h_all[:, b, :, :], h_all[:, b, :, :], row(R_GA, b), ALU.mult).then_inc(res_chain, 1)
                pool.wait_ge(res_chain, b + 1)
                g.tensor_tensor(h_all[:, b, :, :], h_all[:, b, :, :], x_all[:, b, :, :], ALU.add).then_inc(res_done, 1)

            def prepare_rstd(n):
                pool.wait_ge(var3_done, n + 1)
                g.tensor_tensor(rs3[:, :], ve3[:, :], minus_half[:, :], ALU.pow).then_inc(rstd3_done, 1)

            def prepare_u(n):
                pool.wait_ge(z_done, n + 1)
                wait(pool, base_done, n)
                g.tensor_tensor(u[:, :, :], z[:, :, :], row(R_GCB, n), ALU.mult).then_inc(u_chain, 1)
                pool.wait_ge(u_chain, n + 1)
                g.tensor_tensor(u[:, :, :], u[:, :, :], row(R_GSB, n), ALU.add).then_inc(u_done, 1)

            def prepare_lo(n, par):
                pool.wait_ge(h2_hi_done, n + 1)
                g.tensor_tensor(h2_lo[:, par, :], h2t[:, :], h2_hi[:, par, :].bitcast(F32), ALU.subtract).then_inc(h2_lo_done, 1)

            def experts(c, par, has_next):
                for p in range(PAIRS):
                    q = c * PAIRS + p
                    wait(pool, down_mm, q - 3)
                    pool.wait_ge(hi_done, q + 1)
                    g.tensor_tensor(act_lo[:, p % 4, :], act4[:, p % 4, :], act_hi[:, p % 4, :].bitcast(F32),
                                    ALU.subtract).then_inc(lo_done, 1)
                    if has_next and p == 4:
                        prepare_rstd(c + 1)
                    if has_next and p == 7:
                        prepare_u(c + 1)
                    if has_next and p == 9:
                        prepare_lo(c + 1, 1 - par)

            pool.wait_ge(side_out, len(SIDE_WORK))
            prepare_rstd(0)
            prepare_u(0)
            prepare_lo(0, 0)
            experts(0, 0, True)
            with pool.Fori(0, (B - 2) // 2) as i:
                experts(i * 2 + 1, 1, True)
                experts(i * 2 + 2, 0, True)
            experts(B - 1, 1, False)

        @block.scalar
        def _(act):
            a = nc.scalar
            act.dma_start(small[:, 0:S], A).then_inc(in_small, 16)
            act.dma_start(small[:, S:S + P], C).then_inc(in_small, 16)
            act.dma_start(small[:, S + P:S + P + 1], b_delta.unsqueeze(1)).then_inc(in_small, 16)
            act.dma_start(small[:, S + P + 1:S + P + 2], b_in.unsqueeze(1)).then_inc(in_small, 16)
            act.dma_start(w_small[:, 0, :], w_delta).then_inc(in_small, 16)
            act.dma_start(w_small[:, 1, :], w_in).then_inc(in_small, 16)
            act.dma_start(gb_col[:, 0:1], ln_gamma.unsqueeze(1)).then_inc(in_small, 16)
            act.dma_start(gb_col[:, 1:2], ln_beta.unsqueeze(1)).then_inc(in_small, 16)
            act.dma_start(wg_sb[:, :], w_gate).then_inc(in_small, 16)
            act.dma_start(bg_row[:, :], b_gate.unsqueeze(0)).then_inc(in_small, 16)
            act.dma_start(cls_sb[:, :], classifier).then_inc(in_small, 16)
            act.dma_start(route_bias_sb[:, :], route_bias.unsqueeze(0).broadcast_to([P, E_T])).then_inc(in_small, 16)

            act.wait_ge(in_cond, 16)
            a.activation(c_silu[:, :], c_row[:, :], ACT.Silu).then_inc(c_silu_done, 1)
            for k in range(4):
                act.wait_ge(rows_mm, k + 1)
                what, b0 = (R_SA, R_CA1)[k // 2], 4 * (k % 2)
                a.activation(rows[:, what, b0:b0 + 4, :].rearrange("p b d -> p (b d)"),
                             bank[:, SIDE[k] if k else 6, :], ACT.Identity).then_inc(rows_out, 1)
            with act.Fori(0, B) as b:
                wait_apart(act, rstd1_done, b + 1)
                for j in range(NT):
                    done = a.activation(h_all[:, b, j, :], x_all[:, b, j, :], ACT.Identity,
                                        bias=mr1[:, b, j:j + 1], scale=rs1[:, b, j:j + 1])
                done.then_inc(z1_done, 1)

            def normalise(b):
                wait_apart(act, rstd2_done, b + 1)
                for j in range(NT):
                    done = a.activation(xn_all[:, b, j * P:(j + 1) * P], h_all[:, b, j, :], ACT.Identity,
                                        bias=mr2[:, b, j:j + 1], scale=rs2[:, b, j:j + 1])
                done.then_inc(z2_done, 1)

            def affine(b, b_bank):
                wait_apart(act, z2t_done, b + 1)
                a.activation(xn_all[:, b, :], b_bank, ACT.Identity,
                             bias=gb_col[:, 1:2], scale=gb_col[:, 0:1]).then_inc(xnt_done, 1)

            normalise(0)
            normalise(1)
            affine(0, bank[:, MISC[0], :])
            with act.Fori(0, (B - 2) // 2) as i:
                normalise(i * 2 + 2)
                affine(i * 2 + 1, bank[:, MISC[1], :])
                normalise(i * 2 + 3)
                affine(i * 2 + 2, bank[:, MISC[0], :])
            affine(B - 1, bank[:, MISC[1], :])
            act.wait_ge(proj_done, 1)
            a.activation(delta[:, :], bank[:, DELTA_B, :], ACT.Sigmoid, bias=small_rep[:, S + P:S + P + 1]).then_inc(proj_out, 1)
            a.activation(drive[:, :], bank[:, DRIVE_B, :], ACT.Identity, bias=small_rep[:, S + P + 1:S + P + 2]).then_inc(proj_out, 1)

            for n in range(SWEEP_STEPS):
                k = n % SEG_LEN
                act.wait_ge(step_mm, n + 1)
                a.activation(H[:, k::SEG_LEN], bank[:, SCAN[n % 2], 0:SEGS], ACT.Tanh).then_inc(step_h, 1)
                if n < len(SIDE_WORK):
                    kind, m = SIDE_WORK[n]
                    act.wait_ge(side_mm, n + 1)
                    src = bank[:, SIDE[n % 4], :]
                    if kind == "weights":
                        a.activation(w_hi[:, m // 4, 4 * (m % 4):4 * (m % 4) + 4, :].rearrange("p k d -> p (k d)"),
                                     src, ACT.Identity).then_inc(side_hi, 1)
                    elif kind == "gate":
                        a.activation(xn_all[:, m, :], src, ACT.Sigmoid).then_inc(side_out, 1)
                    else:
                        what, _, b0 = ROW_LIST[4 * m]
                        a.activation(rows[:, what, b0:b0 + 4, :].rearrange("p b d -> p (b d)"), src,
                                     ACT.Identity).then_inc(side_out, 1)
            act.wait_ge(verdict, 1)
            go_on = act.value_load(again[0:1, 0:1])
            with act.If(go_on != 0):
                with act.Fori(0, SEGS - 2) as s:
                    with act.Fori(0, SEG_LEN) as k:
                        act.wait_ge(more_mm, s * SEG_LEN + k + 1)
                        a.activation(H[:, bass.ds(k, SEGS, SEG_LEN)], bank[:, SCAN[0], 0:SEGS], ACT.Tanh).then_inc(more_h, 1)

            def prepare_h2(n, par):
                act.wait_ge(zt_mm, n + 1)
                wait(act, h2_lo_done, n)
                a.activation(h2t[:, :], bank[:, MISC[0], :], ACT.Identity,
                             bias=now_mod[:, 0:1], scale=now_mod[:, 1:2]).then_inc(h2t_done, 1)
                act.wait_ge(h2t_done, n + 1)
                a.activation(h2_hi[:, par, :], h2t[:, :], ACT.Identity).then_inc(h2_hi_done, 1)

            def prepare_exp(n):
                act.wait_ge(shifted_done, n + 1)
                a.activation(ex[:, :, :], ls[:, :, :], ACT.Exp).then_inc(exp_done, 1)

            def prepare_w3t(n):
                act.wait_ge(w3t_mm, n + 1)
                wait(act, route_mm, n * PAIRS)
                a.activation(w3t[:, :], bank[0:96, MISC[0], :].bitcast(BF16)[:, 0:512], ACT.Identity).then_inc(w3t_done, 1)

            def leave_down(c):
                act.wait_ge(down_mm, (c + 1) * PAIRS)
                wait(act, ft_mm, c)
                act.wait_ge(gb_ready, c + 1)
                a.activation(f_t[:, :], bank[:, DOWN_B, :], ACT.Identity, scale=now_gb[:, :]).then_inc(f_done, 1)

            def high_part(q, slot):
                wait(act, down_mm, q - 3)
                act.wait_ge(act_done, q + 1)
                a.activation(act_hi[:, slot, :], act4[:, slot, :], ACT.Identity).then_inc(hi_done, 1)

            def experts(c, par, has_prev, has_next):
                for p in range(PAIRS):
                    q = c * PAIRS + p
                    wait(act, gated_done, q - 1)
                    act.wait_ge(gate_mm, q + 1)
                    a.activation(silu_g[:, p % 2, :], bank[:, GATE_B[p % 2], :], ACT.Silu).then_inc(silu_done, 1)
                    if p > 0 or has_prev:
                        high_part(q - 1, (p - 1) % 4)
                    if has_prev and p == 2:
                        leave_down(c - 1)
                    if has_next and p == 8:
                        prepare_h2(c + 1, 1 - par)
                    if has_next and p == 11:
                        prepare_exp(c + 1)
                if has_next:
                    prepare_w3t(c + 1)

            prepare_h2(0, 0)
            prepare_exp(0)
            prepare_w3t(0)
            experts(0, 0, False, True)
            with act.Fori(0, (B - 2) // 2) as i:
                experts(i * 2 + 1, 1, True, True)
                experts(i * 2 + 2, 0, True, True)
            experts(B - 1, 1, True, False)
            high_part(B * PAIRS - 1, (PAIRS - 1) % 4)
            leave_down(B - 1)

        @block.vector
        def _(dve):
            v = nc.vector
            chained = [0]

            def chain(ins):
                chained[0] += 1
                ins.then_inc(dve_chain, 1)
                dve.wait_ge(dve_chain, chained[0])

            v.memset(ones_col[:, :], 1.0)
            v.memset(h_in0[:, :], 0.0)
            v.memset(wd_pad[:, :], 0.0)
            chain(v.memset(wi_pad[:, :], 0.0))
            dve.wait_ge(in_small, 16 * 12)
            v.tensor_copy(wd_pad[:, PAD:P], w_small[:, 0, :])
            v.tensor_copy(wi_pad[:, PAD:P], w_small[:, 1, :]).then_inc(setup_dve, 1)
            dve.wait_ge(setup_mm, 1)
            v.tensor_copy(c_silu_t[:, :], bank[:, SETUP_B, 0:B]).then_inc(setup_dve, 1)
            dve.wait_ge(setup_mm, 2)
            raw = bank[:, SETUP_B, 0:NMOD * B].rearrange("p (m b) -> p m b", m=NMOD)
            v.tensor_copy(modt[:, 0:NMOD, :], raw)
            v.tensor_copy(small_rep[:, :], bank[:, SETUP_B, 64:64 + S + P + 2])
            chain(v.tensor_copy(cls_t[:, :], bank[:, SETUP_B, 256:256 + E_T]))
            for k in (CA1, CB1):
                chain(v.tensor_scalar_add(modt[:, k, :], modt[:, k, :], 1.0))
            for k in (GA, GB):
                chain(v.tensor_scalar(mod_tmp[:, 0, :], modt[:, k, :], 0.0, 2.0, ALU.is_ge, ALU.mult))
                chain(v.tensor_scalar_add(mod_tmp[:, 0, :], mod_tmp[:, 0, :], -1.0))
                chain(v.tensor_tensor(mod_tmp[:, 1, :], modt[:, k, :], mod_tmp[:, 0, :], ALU.mult))
                chain(v.scalar_tensor_tensor(out=modt[:, k, :], in0=mod_tmp[:, 1, :], scalar=MOD_FLOOR,
                                             in1=mod_tmp[:, 0, :], op0=ALU.max, op1=ALU.mult))
            v.tensor_copy(ga_rep[:, :, :], modt[:, GA, :].unsqueeze(2).broadcast_to([P, B, S]))
            v.tensor_tensor(modt[:, GCB, :], modt[:, GB, :], modt[:, CB1, :], ALU.mult)
            v.tensor_tensor(modt[:, GSB, :], modt[:, GB, :], modt[:, SB_, :], ALU.mult).then_inc(setup_dve, 1)
            dve.wait_ge(pool_const, 7)
            v.tensor_tensor(a_block[:, :, :], small_rep[:, 0:S].unsqueeze(1).broadcast_to([P, B, S]),
                            own_batch[:, :].unsqueeze(2).broadcast_to([P, B, S]), ALU.mult)

            def spread(source, done):
                for j in range(NT):
                    last = v.bn_stats(stats[:, j, :], source(j))
                last.then_inc(done, 1)

            def combine(sem_, base_count):
                dve.wait_ge(sem_, base_count)
                v.tensor_tensor(mom[:, 0, :], stats[:, :, 1], stats[:, :, 4], ALU.add)
                v.tensor_tensor(mom[:, 2, :], stats[:, :, 2], stats[:, :, 5], ALU.add)
                v.tensor_tensor(mom[:, 1, :], stats[:, :, 1], stats[:, :, 4], ALU.subtract).then_inc(sem_, 1)
                dve.wait_ge(sem_, base_count + 1)
                v.tensor_tensor(mom[:, 3, :], mom[:, 1, :], mom[:, 1, :], ALU.mult).then_inc(sem_, 1)
                dve.wait_ge(sem_, base_count + 2)
                v.scalar_tensor_tensor(out=mom[:, 4, :], in0=mom[:, 3, :], scalar=P / 4.0, in1=mom[:, 2, :],
                                       op0=ALU.mult, op1=ALU.add).then_inc(sem_, 1)
                dve.wait_ge(sem_, base_count + 3)

            def moments_out(b, ve, nm, done):
                v.tensor_scalar_mul(nm[:, b, :], mom[:, 0, :], -0.5)
                v.tensor_scalar(ve[:, b, :], mom[:, 4, :], 1.0 / P, EPS, ALU.mult, ALU.add).then_inc(done, 1)

            for half in range(2):
                dve.wait_ge(in_x[half], 16 * (B // 2))
                with dve.Fori(half * (B // 2), (half + 1) * (B // 2)) as b:
                    spread(lambda j: x_all[:, b, j, :], mom1_chain)
                    combine(mom1_chain, b * 4 + 1)
                    moments_out(b, ve1, nm1, stats1_done)

            def second_moments(b, previous):
                dve.wait_ge(scaled_done, b + 1)
                v.tensor_tensor(h_all[:, b, :, :], h_all[:, b, :, :], row(R_SA, b), ALU.add).then_inc(h_done, 1)
                dve.wait_ge(h_done, b + 1)
                if previous is not None:
                    moments_out(previous, ve2, nm2, stats2_done)
                spread(lambda j: h_all[:, b, j, :], mom2_chain)
                combine(mom2_chain, b * 4 + 1)

            second_moments(0, None)
            with dve.Fori(1, B) as b:
                second_moments(b, b - 1)
            moments_out(B - 1, ve2, nm2, stats2_done)
            dve.wait_ge(setup_mm, 3)
            chain(v.tensor_copy(ga_t[:, :], bank[:, SETUP_B, 0:P]))
            chain(v.tensor_tensor(c_ga[:, :], small_rep[:, S:S + P], ga_t[:, :], ALU.mult))
            v.tensor_tensor(c_batch[:, :, :], c_ga[:, :].unsqueeze(1).broadcast_to([P, B, P]),
                            own_batch[:, :].unsqueeze(2).broadcast_to([P, B, P]), ALU.mult).then_inc(setup_dve, 1)

            dve.wait_ge(proj_out, 1)
            for n in range(SWEEP_STEPS):
                k = n % SEG_LEN
                dve.wait_ge(step_h, n + 1)
                if k < SEG_LEN - 1:
                    v.tensor_tensor(h_in[:, :], H[:, k::SEG_LEN], delta[:, k + 1::SEG_LEN], ALU.mult).then_inc(step_in, 1)
                elif n < SWEEP_STEPS - 1:
                    v.tensor_tensor(h_in0[:, 1:SEGS], H[:, k:T - SEG_LEN:SEG_LEN], delta[:, SEG_LEN::SEG_LEN],
                                    ALU.mult).then_inc(step_in, 1)
                    v.tensor_copy(ends[:, :], H[:, k::SEG_LEN])
                else:
                    chain(v.tensor_tensor(differ[:, :], H[:, k::SEG_LEN], ends[:, :], ALU.not_equal))
                    v.tensor_reduce(differ_p[:, :], differ[:, :], AX, ALU.max).then_inc(step_in, 1)
                if n < len(SIDE_WORK) and SIDE_WORK[n][0] == "weights":
                    m = SIDE_WORK[n][1]
                    dve.wait_ge(side_hi, m + 1)
                    part = (slice(None), m // 4, slice(4 * (m % 4), 4 * (m % 4) + 4), slice(None))
                    v.tensor_tensor(w_lo[part].rearrange("p k d -> p (k d)"), bank[:, SIDE[n % 4], :],
                                    w_hi[part].rearrange("p k d -> p (k d)").bitcast(F32), ALU.subtract).then_inc(side_out, 1)
            dve.wait_ge(verdict_mm, 1)
            v.tensor_copy(again[:, :], bank[0:1, SCAN[0], 0:1]).then_inc(verdict, 1)
            dve.wait_ge(verdict, 1)
            go_on = dve.value_load(again[0:1, 0:1])
            with dve.If(go_on != 0):
                with dve.Fori(0, SEGS - 2) as s:
                    v.tensor_tensor(h_in[:, 1:SEGS], H[:, SEG_LEN - 1:T - SEG_LEN:SEG_LEN], delta[:, SEG_LEN::SEG_LEN], ALU.mult)
                    v.memset(h_in[:, 0:1], 0.0).then_inc(more_in, 1)
                    with dve.Fori(0, SEG_LEN - 1) as k:
                        dve.wait_ge(more_h, s * SEG_LEN + k + 1)
                        v.tensor_tensor(h_in[:, :], H[:, bass.ds(k, SEGS, SEG_LEN)], delta[:, bass.ds(k + 1, SEGS, SEG_LEN)],
                                        ALU.mult).then_inc(more_in, 1)
                    dve.wait_ge(more_h, s * SEG_LEN + SEG_LEN)

            PRE = 17
            at = [0]

            def link(ins, n):
                at[0] += 1
                ins.then_inc(pre_chain, 1)
                dve.wait_ge(pre_chain, n * PRE + at[0])

            def prepare_x1(n):
                at[0] = 0
                dve.wait_ge(y_mm, n + 1)
                dve.wait_ge(res_done, n + 1)
                wait(dve, base_done, n)
                link(v.tensor_tensor(v_t[:, :, :].rearrange("p j d -> p (j d)"), bank[:, MISC[0], :], xn_all[:, n, :], ALU.mult), n)
                link(v.tensor_tensor(x1[:, :, :], v_t[:, :, :], h_all[:, n, :, :], ALU.add), n)
                spread(lambda j: x1[:, j, :], mom3_chain)
                v.tensor_copy(now_mod[:, :], modt[:, SB_:CB1 + 1, n])
                combine(mom3_chain, n * 4 + 1)
                v.tensor_scalar_mul(mean3[:, :], mom[:, 0, :], 0.5)
                v.tensor_scalar(ve3[:, :], mom[:, 4, :], 1.0 / P, EPS, ALU.mult, ALU.add).then_inc(var3_done, 1)

            def prepare_z(n):
                dve.wait_ge(rstd3_done, n + 1)
                wait(dve, u_done, n)
                for j in range(NT):
                    last = v.tensor_scalar(z[:, j, :], x1[:, j, :], mean3[:, j:j + 1], rs3[:, j:j + 1], ALU.subtract, ALU.mult)
                last.then_inc(z_done, 1)

            def over(t):
                return t.unsqueeze(2).broadcast_to([P, NT, E_T])

            def prepare_shift(n):
                dve.wait_ge(logit_mm, n + 1)
                logits = bank[:, MISC[1], 0:NT * E_T].rearrange("p (j e) -> p j e", j=NT)
                link(v.tensor_reduce(lmax[:, :], logits, AX, ALU.max), n)
                v.tensor_tensor(ls[:, :, :], logits, over(lmax[:, :]), ALU.subtract).then_inc(shifted_done, 1)

            def prepare_scores(n):
                dve.wait_ge(exp_done, n + 1)
                link(v.tensor_reduce(esum[:, :], ex[:, :, :], AX, ALU.add), n)
                link(v.reciprocal(erec[:, :], esum[:, :]), n)
                link(v.tensor_tensor(score[:, :, :], ex[:, :, :], over(erec[:, :]), ALU.mult), n)
                link(v.tensor_tensor(biased[:, :, :], score[:, :, :],
                                     route_bias_sb[:, :].unsqueeze(1).broadcast_to([P, NT, E_T]), ALU.add), n)

            def prepare_top(n):
                v.tensor_scalar_mul(scaled[:, :, :], score[:, :, :], ROUTE_SCALE)
                for j in range(NT):
                    last = v.max(top8[:, j, :], biased[:, j, :])
                link(last, n)
                v.tensor_tensor(at_or_above[:, :, :], biased[:, :, :], over(top8[:, :, TOP_K - 1]), ALU.is_ge)
                for j in range(NT):
                    last = v.max_index(top8_at[:, j, :], top8[:, j, :], biased[:, j, :])
                link(last, n)

            def prepare_weights(n):
                link(v.tensor_copy(last_at[:, :], top8_at[:, :, TOP_K - 1]), n)
                sixth = over(top8[:, :, TOP_K - 1])
                v.tensor_tensor(above[:, :, :], biased[:, :, :], sixth, ALU.is_gt)
                link(v.tensor_tensor(early[:, :, :], expert_no[:, :].unsqueeze(1).broadcast_to([P, NT, E_T]),
                                     over(last_at[:, :]), ALU.is_le), n)
                link(v.tensor_tensor(above[:, :, :], above[:, :, :], early[:, :, :], ALU.max), n)
                link(v.tensor_tensor(above[:, :, :], above[:, :, :], at_or_above[:, :, :], ALU.mult), n)
                link(v.tensor_tensor(weight[:, :, :], above[:, :, :], scaled[:, :, :], ALU.mult), n)

            def prepare_split(n):
                v.tensor_reduce(zero_w[:, :], weight[:, :, E_R:E_T], AX, ALU.add)
                link(v.tensor_copy(w3[:, :, 0, :], weight[:, :, 0:E_R]), n)
                link(v.tensor_tensor(rest1[:, :, :], weight[:, :, 0:E_R], w3[:, :, 0, :], ALU.subtract), n)
                link(v.tensor_copy(w3[:, :, 1, :], rest1[:, :, :]), n)
                v.tensor_tensor(w3[:, :, 2, :], rest1[:, :, :], w3[:, :, 1, :], ALU.subtract).then_inc(w3_done, 1)

            def make_base(c, par):
                dve.wait_ge(u_done, c + 1)
                dve.wait_ge(w3_done, c + 1)
                for j in range(NT):
                    last = v.scalar_tensor_tensor(out=base[:, par, j, :], in0=u[:, j, :], scalar=zero_w[:, j:j + 1],
                                                  in1=x1[:, j, :], op0=ALU.mult, op1=ALU.add)
                last.then_inc(base_done, 1)

            def prepare_gb(c):
                wait(dve, f_done, c)
                v.tensor_scalar_mul(now_gb[:, :], modt[:, GB, bass.ds(c, 1)], 1.0).then_inc(gb_ready, 1)

            def finish(c, par):
                dve.wait_ge(ft_mm, c + 1)
                dve.wait_ge(base_done, c + 1)
                wait(dve, out_dma, 16 * c)
                v.tensor_tensor(out_sb[:, :, :].rearrange("p j d -> p (j d)"), bank[:, MISC[1], :],
                                base[:, par, :, :].rearrange("p j d -> p (j d)"), ALU.add).then_inc(out_ready, 1)

            def experts(c, par, has_prev, has_next):
                for p in range(PAIRS):
                    q = c * PAIRS + p
                    dve.wait_ge(silu_done, q + 1)
                    dve.wait_ge(up_mm, q + 1)
                    wait(dve, act_done, q - 1)
                    v.tensor_tensor(gated[:, p % 2, :], silu_g[:, p % 2, :], bank[:, UP_B[p % 2], :], ALU.mult).then_inc(gated_done, 1)
                    dve.wait_ge(gated_done, q + 1)
                    dve.wait_ge(route_mm, q + 1)
                    wait(dve, lo_done, q - 3)
                    v.tensor_tensor(act4[:, p % 4, :], gated[:, p % 2, :], bank[:, ROUTE_B, :], ALU.mult).then_inc(act_done, 1)
                    if p == 0:
                        make_base(c, par)
                    if has_next and p == 3:
                        prepare_x1(c + 1)
                    if has_prev and p == 4:
                        finish(c - 1, 1 - par)
                    if has_next and p == 5:
                        prepare_z(c + 1)
                    if p == 6:
                        prepare_gb(c)
                    if has_next and p == 10:
                        prepare_shift(c + 1)
                    if has_next and p == 12:
                        prepare_scores(c + 1)
                        prepare_top(c + 1)
                    if has_next and p == 13:
                        prepare_weights(c + 1)
                    if has_next and p == 14:
                        prepare_split(c + 1)
                        assert at[0] == PRE

            dve.wait_ge(side_out, len(SIDE_WORK))
            dve.wait_ge(res_done, B)
            prepare_x1(0)
            prepare_z(0)
            prepare_shift(0)
            prepare_scores(0)
            prepare_top(0)
            prepare_weights(0)
            prepare_split(0)
            assert at[0] == PRE, at[0]
            experts(0, 0, False, True)
            with dve.Fori(0, (B - 2) // 2) as i:
                experts(i * 2 + 1, 1, True, True)
                experts(i * 2 + 2, 0, True, True)
            experts(B - 1, 1, True, False)
            finish(B - 1, 1)

        @block.tensor
        def _(pe):
            mm = nc.tensor.matmul
            pe.wait_ge(pool_const, 11)
            pe.wait_ge(c_silu_done, 1)
            nc.tensor.transpose(bank[:, SETUP_B, 0:B], c_silu[:, :], ident[0:B, 0:B]).then_inc(setup_mm, 1)
            pe.wait_ge(setup_dve, 2)
            pe.wait_ge(in_wmod, 16)
            pe.wait_ge(in_small, 16 * 12)
            for m in range(NMOD):
                mm(bank[:, SETUP_B, m * B:(m + 1) * B], wmod_sb[:, m * P:(m + 1) * P], c_silu_t[:, :], start=True, stop=True)
            mm(bank[:, SETUP_B, 64:64 + S + P + 2], every_batch[:, :, :].rearrange("k b s -> k (b s)"), small[:, :],
               start=True, stop=True)
            nc.tensor.transpose(bank[:, SETUP_B, 256:256 + E_T], cls_sb[:, :], ident[0:E_T, 0:E_T]).then_inc(setup_mm, 1)
            pe.wait_ge(setup_dve, 3)

            def broadcast_row(dst, k, b):
                return mm(dst, modt[:, k, b:b + 1].broadcast_to([P, P]), ident[:, :], start=True, stop=True)

            for k in range(4):
                to = bank[:, SIDE[k] if k else 6, :]
                for r in range(4):
                    done = broadcast_row(to[:, r * P:(r + 1) * P], (SA, CA1)[k // 2], 4 * (k % 2) + r)
                done.then_inc(rows_mm, 1)
            mm(bank[:, SETUP_B, 0:P], ga_rep[:, :, :].rearrange("d b s -> d (b s)"), ident[:, :],
               start=True, stop=True).then_inc(setup_mm, 1)

            pe.wait_ge(rows_out, 4)
            pe.wait_ge(setup_dve, 1)

            def project(b):
                pe.wait_ge(xnt_done, b + 1)
                lo = PAD - S * b
                mm(bank[:, DELTA_B, :], wd_pad[:, lo:lo + P], xn_all[:, b, :], start=b == 0, stop=b == B - 1)
                return mm(bank[:, DRIVE_B, :], wi_pad[:, lo:lo + P], xn_all[:, b, :], start=b == 0, stop=b == B - 1)

            for b in range(B):
                pe.wait_ge(z2_done, b + 1)
                wait(pe, xnt_done, b - 1)
                for j in range(NT):
                    done = nc.tensor.transpose(bank[:, MISC[b % 2], j * P:(j + 1) * P], xn_all[:, b, j * P:(j + 1) * P], ident[:, :])
                done.then_inc(z2t_done, 1)
                if b:
                    project(b - 1)
            project(B - 1).then_inc(proj_done, 1)

            def seed(n, dst, k, last):
                return mm(dst, ident[:, :], drive[:, k::SEG_LEN], start=True, stop=last)

            def side(n):
                kind, m = SIDE_WORK[n]
                to = bank[:, SIDE[n % 4], :]
                wait(pe, side_out, n - 3)
                if kind == "weights":
                    which, g = m // 4, m % 4
                    pe.wait_ge(in_dn if which == 2 else in_gu, 16 if which == 2 else 64)
                    for r in range(4):
                        pair = 4 * g + r
                        src = (dn_raw[:, 2 * pair:2 * pair + 2, :].rearrange("h e i -> h (e i)") if which == 2
                               else gu_raw[:, which, pair, :])
                        done = nc.tensor.transpose(to[:, r * P:(r + 1) * P], src, ident[:, :])
                elif kind == "gate":
                    mm(to, ones_row[:, :], bg_row[:, :].unsqueeze(1).broadcast_to([1, NT, P]), start=True, stop=True)
                    for j in range(NT):
                        done = mm(to[:, j * P:(j + 1) * P], xn_all[:, m, j * P:(j + 1) * P], wg_sb[:, :],
                                  start=False, stop=True, skip_group_check=True)
                else:
                    for r in range(4):
                        _, k, b = ROW_LIST[4 * m + r]
                        done = broadcast_row(to[:, r * P:(r + 1) * P], k, b)
                done.then_inc(side_mm, 1)

            pe.wait_ge(proj_out, 2)
            pe.wait_ge(setup_dve, 4)
            seed(0, bank[:, SCAN[0], 0:SEGS], 0, True).then_inc(step_mm, 1)
            for n in range(1, SWEEP_STEPS):
                k = n % SEG_LEN
                dst = bank[:, SCAN[n % 2], 0:SEGS]
                seed(n, dst, k, False)
                if n - 1 < len(SIDE_WORK):
                    side(n - 1)
                pe.wait_ge(step_in, n)
                mm(dst, a_block[:, :, :].rearrange("p b s -> p (b s)"), (h_in if k else h_in0)[:, :],
                   start=False, stop=True).then_inc(step_mm, 1)
            pe.wait_ge(step_in, SWEEP_STEPS)
            mm(bank[0:1, SCAN[0], 0:1], differ_p[:, :], ones_col[:, :], start=True, stop=True).then_inc(verdict_mm, 1)
            pe.wait_ge(verdict, 1)
            go_on = pe.value_load(again[0:1, 0:1])
            with pe.If(go_on != 0):
                with pe.Fori(0, SEGS - 2) as s:
                    with pe.Fori(0, SEG_LEN) as k:
                        pe.wait_ge(more_in, s * SEG_LEN + k + 1)
                        mm(bank[:, SCAN[0], 0:SEGS], ident[:, :], drive[:, bass.ds(k, SEGS, SEG_LEN)], start=True, stop=False)
                        mm(bank[:, SCAN[0], 0:SEGS], a_block[:, :, :].rearrange("p b s -> p (b s)"), h_in[:, :],
                           start=False, stop=True).then_inc(more_mm, 1)
                pe.wait_ge(more_h, (SEGS - 2) * SEG_LEN)

            def prepare_y(n):
                for j in range(NT):
                    done = mm(bank[:, MISC[0], j * P:(j + 1) * P], H[:, j * P:(j + 1) * P], c_batch[:, n, :], start=True, stop=True)
                done.then_inc(y_mm, 1)

            def prepare_zt(n):
                pe.wait_ge(z_done, n + 1)
                for j in range(NT):
                    done = nc.tensor.transpose(bank[:, MISC[0], j * P:(j + 1) * P], z[:, j, :], ident[:, :])
                done.then_inc(zt_mm, 1)

            def prepare_logits(n):
                pe.wait_ge(h2t_done, n + 1)
                wait(pe, out_ready, n - 1)
                for j in range(NT):
                    done = mm(bank[:, MISC[1], j * E_T:(j + 1) * E_T], h2t[:, j * P:(j + 1) * P], cls_t[:, :], start=True, stop=True)
                done.then_inc(logit_mm, 1)

            def prepare_w3t(n):
                pe.wait_ge(w3_done, n + 1)
                to = bank[0:96, MISC[0], :].bitcast(BF16)
                for j in range(NT):
                    done = nc.tensor.transpose(to[:, j * P:(j + 1) * P], w3[:, j, :, :].rearrange("p k e -> p (k e)"), ident_bf[:, :])
                done.then_inc(w3t_mm, 1)

            def split_product(dst, which, pair, hi, lo, first=True, last=True):
                mm(dst, w_hi[:, which, pair, :], hi, start=first, stop=False)
                mm(dst, w_hi[:, which, pair, :], lo, start=False, stop=False)
                return mm(dst, w_lo[:, which, pair, :], hi, start=False, stop=last)

            def down_product(c, p):
                q = c * PAIRS + p
                if p == 0:
                    wait(pe, f_done, c)
                pe.wait_ge(lo_done, q + 1)
                pe.wait_ge(hi_done, q + 1)
                split_product(bank[:, DOWN_B, :], 2, p, act_hi[:, p % 4, :], act_lo[:, p % 4, :],
                              p == 0, p == PAIRS - 1).then_inc(down_mm, 1)

            def transpose_down(c):
                pe.wait_ge(f_done, c + 1)
                for j in range(NT):
                    done = nc.tensor.transpose(bank[:, MISC[1], j * P:(j + 1) * P], f_t[:, j * P:(j + 1) * P], ident[:, :])
                done.then_inc(ft_mm, 1)

            def experts(c, par, has_prev, has_next):
                for p in range(PAIRS):
                    q = c * PAIRS + p
                    if p == 0:
                        pe.wait_ge(h2_lo_done, c + 1)
                    wait(pe, silu_done, q - 1)
                    split_product(bank[:, GATE_B[p % 2], :], 0, p, h2_hi[:, par, :], h2_lo[:, par, :]).then_inc(gate_mm, 1)
                    wait(pe, gated_done, q - 1)
                    split_product(bank[:, UP_B[p % 2], :], 1, p, h2_hi[:, par, :], h2_lo[:, par, :]).then_inc(up_mm, 1)
                    if p == 0:
                        pe.wait_ge(w3t_done, c + 1)
                    wait(pe, act_done, q)
                    mm(bank[:, ROUTE_B, :], pick_pair[:, p, :], w3t[:, :], start=True, stop=True).then_inc(route_mm, 1)
                    if p >= 2:
                        down_product(c, p - 2)
                    elif has_prev:
                        down_product(c - 1, PAIRS - 2 + p)
                    if has_next and p == 1:
                        prepare_y(c + 1)
                    if has_prev and p == 3:
                        transpose_down(c - 1)
                    if has_next and p == 7:
                        prepare_zt(c + 1)
                    if has_next and p == 9:
                        prepare_logits(c + 1)
                if has_next:
                    prepare_w3t(c + 1)

            pe.wait_ge(pool_const, N_POOL_CONST)
            pe.wait_ge(side_out, len(SIDE_WORK))
            prepare_y(0)
            prepare_zt(0)
            prepare_logits(0)
            prepare_w3t(0)
            experts(0, 0, False, True)
            with pe.Fori(0, (B - 2) // 2) as i:
                experts(i * 2 + 1, 1, True, True)
                experts(i * 2 + 2, 0, True, True)
            experts(B - 1, 1, True, False)
            down_product(B - 1, PAIRS - 2)
            down_product(B - 1, PAIRS - 1)
            transpose_down(B - 1)


_INS = ['L0_attn_x', 'L0_attn_ln_gamma', 'L0_attn_ln_beta', 'L0_attn_A', 'L0_attn_C', 'L0_attn_w_delta',
        'L0_attn_b_delta', 'L0_attn_w_in', 'L0_attn_b_in', 'L0_attn_w_gate', 'L0_attn_b_gate',
        'L0_ffn_classifier_weight', 'L0_ffn_e_score_correction_bias', 'L0_ffn_gate_up_proj', 'L0_ffn_down_proj',
        'L0_c', 'L0_wmod']


def kernel(**inputs):
    import numpy as _np
    import concourse.bacc as _bacc
    from concourse import mybir as _mybir
    from concourse.bass_utils import run_bass_kernel_spmd as _run

    nc = _bacc.Bacc("TRN2", target_bir_lowering=False, num_devices=1)
    arrays, args = {}, []
    for name in _INS:
        a = _np.ascontiguousarray(inputs[name])
        arrays[f"in_{name}_dram"] = a
        args.append(nc.dram_tensor(f"in_{name}_dram", a.shape, _mybir.dt.from_np(a.dtype), kind="ExternalInput").ap())
    shape = inputs['L0_attn_x'].shape
    args.append(nc.dram_tensor("out_0_dram", shape, F32, kind="ExternalOutput").ap())
    adaln_block(nc, *args)
    r = _run(nc, [arrays], core_ids=[0])
    return r.results[0]["out_0_dram"]
```

```python
from contextlib import ExitStack

import concourse.bass as bass
from concourse import mybir

F32 = mybir.dt.float32
F32R = mybir.dt.float32r
BF16 = mybir.dt.bfloat16
I32 = mybir.dt.int32
U32 = mybir.dt.uint32
ALU = mybir.AluOpType
ACT = mybir.ActivationFunctionType
AX = mybir.AxisListType.X

P = 128
EPS = 1e-5
TOP_K = 6
ROUTE_SCALE = 2.5
MOD_FLOOR = 0.25


def adaln_block(nc, x, ln_gamma, ln_beta, A, C, w_delta, b_delta, w_in, b_in, w_gate, b_gate,
                classifier, route_bias, gate_up, down, cond, wmod, out):
    B, T, D = x.shape
    S = A.shape[0]
    NT = T // P
    SEG_LEN = 16
    SEGS = T // SEG_LEN
    E_T = classifier.shape[0]
    E_R = down.shape[0]
    INNER = down.shape[2]
    GROUPS = 2
    BG = B // GROUPS
    PAIRS = E_R // 2
    NMOD = wmod.shape[1] // D
    assert D == P and BG * 2 * S == P and 2 * INNER == P and NT * P == 512 and gate_up.shape[1] == 2 * INNER

    with ExitStack() as ctx:
        def sb(name, shape, dt=F32):
            return ctx.enter_context(nc.sbuf_tensor(name, shape, dt))

        def sem(name):
            return ctx.enter_context(nc.semaphore(name))

        bank = ctx.enter_context(nc.psum_tensor("bank", [P, 8, 512], F32))
        SCAN = (0, 1)
        SIDE = (2, 3, 4, 5, 6, 7)
        GATE_B, UP_B = (0, 1), (2, 3)
        ROUTE_B = (4, 5)
        DOWN_B = 6
        PREP_B = 7
        MISC = (6, 7)
        PROJ_B = (0, 1)
        SETUP_B = 2
        AT_SMALL, AT_GA, AT_CLS = 64, 64 + S + P + 1, 64 + S + P + 1 + 2 * P
        ROWS_B = (3, 4, 5, 6, 7, 1)

        ident = sb("ident", [P, P + S])
        ident_bf = sb("ident_bf", [P, P], BF16)
        ones3 = sb("ones3", [3, P], BF16)
        own_batch = sb("own_batch", [P, BG])
        spread_rows = sb("spread_rows", [S, 2, BG, 2, S])
        minus_half = sb("minus_half", [P, NT])
        minus_one = sb("minus_one", [P, NT])
        eps = sb("eps", [P, NT])
        warm = sb("warm", [P, 3])
        expert_no = sb("expert_no", [P, E_T])
        W_ROWS = 3 * (E_R + 1)
        pick_pair = sb("pick_pair", [W_ROWS, PAIRS, P], BF16)
        pick_zero = sb("pick_zero", [W_ROWS, P], BF16)

        c_row = sb("c_row", [B, P])
        c_silu = sb("c_silu", [B, P])
        c_silu_t = sb("c_silu_t", [P, B])
        wmod_sb = sb("wmod_sb", [P, NMOD * P])
        SA, CA1, GA, SB_, CB1, GB = range(6)
        modt = sb("modt", [P, NMOD, B])
        mod_tmp = sb("mod_tmp", [P, 2, 2, B])
        R_SA, R_CA1, R_GA = range(3)
        rows = sb("rows", [P, 3, B, P])

        small = sb("small", [S, S + P + 2])
        small_rep = sb("small_rep", [P, S + P + 1])
        a_block = sb("a_block", [P, BG, 2, S])
        c_ga = sb("c_ga", [P, GROUPS, P])
        ga_rep = sb("ga_rep", [P, GROUPS, BG, 2 * S])
        c_batch = sb("c_batch", [P, B, P])
        W_PAD = P - 2 * S
        w_pad = sb("w_pad", [P, 2 * W_PAD + 2 * S])
        gb_col = sb("gb_col", [P, 2])
        wg_sb = sb("wg_sb", [P, P])
        bg3 = sb("bg3", [3, P])
        bg_part = sb("bg_part", [3, 3, P], BF16)
        bg_rest = sb("bg_rest", [3, 2, P])
        bg_mix = sb("bg_mix", [3, P])
        bg_rows = sb("bg_rows", [3, P], BF16)
        cls_sb = sb("cls_sb", [E_T, P])
        cls_t = sb("cls_t", [P, E_T])
        route_bias_sb = sb("route_bias_sb", [P, E_T])

        x_all = sb("x_all", [P, B, NT, P])
        h_all = sb("h_all", [P, B, NT, P])
        xn_all = sb("xn_all", [P, B, 512])
        stats1 = sb("stats1", [P, 2, NT, 6])
        stats2 = sb("stats2", [P, 2, NT, 6])
        stats = sb("stats", [P, NT, 6])
        mv = sb("mv", [P, 2, 2, NT, 2])
        ve = sb("ve", [P, 2, 2, NT])
        nm = sb("nm", [P, 2, 2, NT])
        rs = sb("rs", [P, 2, 2, NT])
        mr = sb("mr", [P, 2, 2, NT])

        COLS = GROUPS * SEGS
        delta = sb("delta", [P, GROUPS * T])
        drive = sb("drive", [P, GROUPS * T])
        H = sb("H", [P, GROUPS * T])
        h_in = sb("h_in", [P, COLS])
        h_in0 = sb("h_in0", [P, COLS])
        ends = sb("ends", [P, COLS])
        differ = sb("differ", [P, COLS])
        differ_p = sb("differ_p", [P, 1])
        ones_col = sb("ones_col", [P, 1])
        again = sb("again", [1, 1], I32)

        gu_raw = sb("gu_raw", [P, 2, PAIRS, P])
        dn_raw = sb("dn_raw", [P, E_R, INNER])
        w_hi = sb("w_hi", [P, 3, PAIRS, P], F32R)
        w_lo = sb("w_lo", [P, 3, PAIRS, P], F32R)

        z = x_all[:, 1, :, :]
        h2t = x_all[:, 3, :, :].rearrange("p j d -> p (j d)")
        raw_g = gu_raw[:, 0, :, :].rearrange("p k d -> p (k d)")
        raw_u = gu_raw[:, 1, :, :].rearrange("p k d -> p (k d)")
        raw_d = dn_raw[:, :, :].rearrange("p e i -> p (e i)")
        act4 = raw_g.rearrange("p (k n) -> p k n", k=4)
        silu_g = raw_u[:, 0:1024].rearrange("p (k n) -> p k n", k=2)
        f_t = raw_u[:, 1024:1536]
        zero_part = raw_d[:, 0:1024].rearrange("p (k n) -> p k n", k=2)
        out_sb = raw_d[:, 1024:1536].rearrange("p (j d) -> p j d", j=NT)
        v_t = raw_d[:, 1536:2048].rearrange("p (j d) -> p j d", j=NT)
        now_mod = sb("now_mod", [P, 2])
        now_gb = sb("now_gb", [P, 2])
        mv3 = sb("mv3", [P, NT, 2])
        ve3 = sb("ve3", [P, NT])
        nm3 = sb("nm3", [P, NT])
        mr3 = sb("mr3", [P, NT])
        rs3 = sb("rs3", [P, NT])
        h2_hi = sb("h2_hi", [P, 2, 512], F32R)
        h2_lo = sb("h2_lo", [P, 2, 512], F32R)
        lmax = sb("lmax", [P, NT])
        ls = sb("ls", [P, NT, E_T])
        ex = sb("ex", [P, NT, E_T])
        esum = sb("esum", [P, NT])
        erec = sb("erec", [P, NT])
        score = sb("score", [P, NT, E_T])
        scaled = sb("scaled", [P, NT, E_T])
        biased = sb("biased", [P, NT, E_T])
        top8 = sb("top8", [P, NT, 8])
        top8_at = sb("top8_at", [P, NT, 8], U32)
        last_at = sb("last_at", [P, NT])
        above = sb("above", [P, NT, E_T])
        at_or_above = sb("at_or_above", [P, NT, E_T])
        early = sb("early", [P, NT, E_T])
        weight = sb("weight", [P, NT, E_T])
        zero_w = sb("zero_w", [P, NT])
        rest1 = sb("rest1", [P, NT, E_R + 1])
        w3 = sb("w3", [P, NT, 3, E_R + 1], BF16)
        w3t = sb("w3t", [W_ROWS, 512], BF16)
        act_hi = sb("act_hi", [P, 4, 512], F32R)
        gated = sb("gated", [P, 2, 512])
        act_lo = sb("act_lo", [P, 4, 512], F32R)

        in_cond = sem("in_cond")
        in_wmod = sem("in_wmod")
        in_small = sem("in_small")
        in_x = sem("in_x")
        in_affine = sem("in_affine")
        in_w = sem("in_w")
        in_late = sem("in_late")
        in_gu = sem("in_gu")
        in_dn = sem("in_dn")
        pool_const = sem("pool_const")
        c_silu_done = sem("c_silu_done")
        ct_mm = sem("ct_mm")
        ct_done = sem("ct_done")
        mod_mm = sem("mod_mm")
        w_pad_done = sem("w_pad_done")
        scale_done = sem("scale_done")
        ga_done = sem("ga_done")
        ga_rep_mm = sem("ga_rep_mm")
        bg_done = sem("bg_done")
        small_done = sem("small_done")
        rows_mm = sem("rows_mm")
        rows_out = sem("rows_out")
        dve_chain = sem("dve_chain")
        moments1 = sem("moments1")
        shape1 = sem("shape1")
        pow1_done = sem("pow1_done")
        rstd1_done = sem("rstd1_done")
        z1_done = sem("z1_done")
        spread1 = sem("spread1")
        spread2 = sem("spread2")
        h_chain = sem("h_chain")
        h_done = sem("h_done")
        moments2 = sem("moments2")
        shape2 = sem("shape2")
        pow2_done = sem("pow2_done")
        rstd2_done = sem("rstd2_done")
        z2_done = sem("z2_done")
        z2t_done = sem("z2t_done")
        xnt_done = sem("xnt_done")
        proj_done = sem("proj_done")
        delta_out = sem("delta_out")
        drive_out = sem("drive_out")
        step_mm = sem("step_mm")
        step_h = sem("step_h")
        step_in = sem("step_in")
        verdict_mm = sem("verdict_mm")
        verdict = sem("verdict")
        more_mm = sem("more_mm")
        more_h = sem("more_h")
        more_in = sem("more_in")
        side_mm = sem("side_mm")
        side_hi = sem("side_hi")
        side_lo = sem("side_lo")
        side_gate = sem("side_gate")
        res_chain = sem("res_chain")
        res_done = sem("res_done")

        gate_mm = sem("gate_mm")
        up_mm = sem("up_mm")
        route_mm = sem("route_mm")
        down_mm = sem("down_mm")
        silu_done = sem("silu_done")
        gated_done = sem("gated_done")
        act_done = sem("act_done")
        hi_done = sem("hi_done")
        lo_done = sem("lo_done")
        y_mm = sem("y_mm")
        zt_mm = sem("zt_mm")
        logit_mm = sem("logit_mm")
        w3t_mm = sem("w3t_mm")
        ft_mm = sem("ft_mm")
        pre_chain = sem("pre_chain")
        var3_done = sem("var3_done")
        rstd3_done = sem("rstd3_done")
        z_done = sem("z_done")
        v_done = sem("v_done")
        x1_done = sem("x1_done")
        stats3_done = sem("stats3_done")
        nm3_done = sem("nm3_done")
        pow3_done = sem("pow3_done")
        zero_mm = sem("zero_mm")
        zero_done = sem("zero_done")
        h2t_done = sem("h2t_done")
        h2_hi_done = sem("h2_hi_done")
        h2_lo_done = sem("h2_lo_done")
        shifted_done = sem("shifted_done")
        exp_done = sem("exp_done")
        w3_done = sem("w3_done")
        w3t_done = sem("w3t_done")
        f_done = sem("f_done")
        gb_ready = sem("gb_ready")
        out_ready = sem("out_ready")
        out_dma = sem("out_dma")

        out_tiles = out.rearrange("b (j p) d -> b p j d", p=P)
        gu_view = gate_up[0:E_R].rearrange("(pair e2) (gu i) h -> e2 gu i pair h", e2=2, gu=2)
        N_SETUP_CONST, N_POOL_CONST = 11, 23

        def wait(eng, s, value):
            if isinstance(value, int) and value <= 0:
                return
            eng.wait_ge(s, value)

        def wait_apart(eng, s, value):
            eng.wait_ge(in_x, 16 * 4)
            eng.wait_ge(s, value)

        def row(k, b):
            return rows[:, k, b, :].unsqueeze(1).broadcast_to([P, NT, P])

        SIDE_WORK = [("weights", n) for n in range(3 * PAIRS // 4)] + [("gate", n) for n in range(2 * B)]
        NS = len(SIDE)
        N_WEIGHTS, N_GATES = 3 * PAIRS // 4, 2 * B

        def side_read(n):
            return (side_lo, n + 1) if n < N_WEIGHTS else (side_gate, n + 1 - N_WEIGHTS)
        ROW_ORDER = [(R_CA1, CA1, 0), (R_SA, SA, 0), (R_CA1, CA1, 1), (R_SA, SA, 1), (R_GA, GA, 0), (R_GA, GA, 1)]
        SWEEP_STEPS = 2 * SEG_LEN

        block = ctx.enter_context(nc.Block())

        @block.sync
        def _(sp):
            for k in range(4):
                sp.dma_start(x_all[:, 2 * k:2 * k + 2, :, :].rearrange("p b j d -> p (b j) d"),
                             x[2 * k:2 * k + 2].rearrange("b (j p) d -> p (b j) d", p=P)).then_inc(in_x, 16)
            sp.dma_start(gb_col[:, 0:1], ln_gamma.unsqueeze(1)).then_inc(in_affine, 16)
            sp.dma_start(gb_col[:, 1:2], ln_beta.unsqueeze(1)).then_inc(in_affine, 16)
            sp.dma_start(wg_sb[:, :], w_gate).then_inc(in_late, 16)
            sp.dma_start(bg3[:, :], b_gate.unsqueeze(0).broadcast_to([3, P])).then_inc(in_late, 16)
            sp.dma_start(cls_sb[:, :], classifier).then_inc(in_late, 16)
            sp.dma_start(route_bias_sb[:, :], route_bias.unsqueeze(0).broadcast_to([P, E_T])).then_inc(in_late, 16)
            for e2 in range(2):
                for gu in range(2):
                    sp.dma_start(gu_raw[e2 * INNER:(e2 + 1) * INNER, gu, :, :], gu_view[e2, gu]).then_inc(in_gu, 16)
            sp.dma_start(dn_raw[:, :, :], down.rearrange("e h i -> h e i")).then_inc(in_dn, 16)
            with sp.Fori(0, B) as b:
                sp.wait_ge(out_ready, b + 1)
                sp.dma_start(out_tiles[bass.ds(b, 1)].rearrange("a p j d -> p (a j) d"), out_sb[:, :, :]).then_inc(out_dma, 16)
            sp.wait_ge(out_dma, 16 * B)

        @block.gpsimd
        def _(pool):
            g = nc.gpsimd
            made = [0]

            def const(ins):
                ins.then_inc(pool_const, 1)
                made[0] += 1
                pool.wait_ge(pool_const, made[0])

            const(g.memset(ident[:, :], 0.0))
            const(g.affine_select(out=ident[:, :], in_=ident[:, :], compare_op=ALU.not_equal, fill=1.0, base=0,
                                  pattern=[[-1, P + S]], channel_multiplier=1))
            const(g.memset(minus_half[:, :], -0.5))
            const(g.memset(minus_one[:, :], -1.0))
            const(g.memset(eps[:, :], EPS))
            const(g.memset(spread_rows[:, :, :, :, :], 0.0))
            for which in range(2):
                const(g.tensor_copy(spread_rows[:, which, :, which, :], ident[0:S, 0:S].unsqueeze(1).broadcast_to([S, BG, S])))
            const(g.memset(own_batch[:, :], 1.0))
            const(g.affine_select(out=own_batch[:, :], in_=own_batch[:, :], compare_op=ALU.is_ge, fill=0.0, base=0,
                                  pattern=[[-2 * S, BG]], channel_multiplier=1))
            const(g.affine_select(out=own_batch[:, :], in_=own_batch[:, :], compare_op=ALU.is_ge, fill=0.0, base=2 * S - 1,
                                  pattern=[[2 * S, BG]], channel_multiplier=-1))
            assert made[0] == N_SETUP_CONST
            const(g.memset(ones3[:, :], 1.0))
            const(g.memset(h_in0[:, :], 0.0))
            const(g.tensor_copy(ident_bf[:, :], ident[:, 0:P]))
            const(g.iota(expert_no[:, :], pattern=[[1, E_T]], base=0, channel_multiplier=0,
                         allow_small_or_imprecise_dtypes=True))
            const(g.memset(pick_pair[:, :, :], 0.0))

            def select_pairs(part):
                at = pick_pair[:, :, :].rearrange("r pair (e2 i) -> r pair e2 i", e2=2)
                const(g.affine_select(out=at, in_=at, compare_op=ALU.not_equal, fill=1.0, base=-(E_R + 1) * part,
                                      pattern=[[-2, PAIRS], [-1, 2], [0, INNER]], channel_multiplier=1))

            select_pairs(0)
            select_pairs(1)

            def rstd(norm, par, b, before, shape, powed, done, used):
                pool.wait_ge(before, b + 1)
                wait(pool, used, b - 1)
                g.tensor_tensor(ve[:, norm, par, :], mv[:, norm, par, :, 1], eps[:, :], ALU.add)
                g.tensor_tensor(nm[:, norm, par, :], mv[:, norm, par, :, 0], minus_one[:, :], ALU.mult).then_inc(shape, 1)
                pool.wait_ge(shape, b + 1)
                g.tensor_tensor(rs[:, norm, par, :], ve[:, norm, par, :], minus_half[:, :], ALU.pow).then_inc(powed, 1)
                pool.wait_ge(powed, b + 1)
                g.tensor_tensor(mr[:, norm, par, :], nm[:, norm, par, :], rs[:, norm, par, :], ALU.mult).then_inc(done, 1)

            def first(b, par):
                rstd(0, par, b, moments1, shape1, pow1_done, rstd1_done, z1_done)

            def second(b, par):
                rstd(1, par, b, moments2, shape2, pow2_done, rstd2_done, z2_done)

            first(0, 0)
            first(1, 1)
            first(2, 0)
            second(0, 0)
            first(3, 1)
            second(1, 1)
            first(4, 0)
            with pool.Fori(1, (B - 4) // 2) as i:
                second(i * 2, 0)
                first(i * 2 + 3, 1)
                second(i * 2 + 1, 1)
                first(i * 2 + 4, 0)
            second(B - 4, 0)
            first(B - 1, 1)
            for b in range(B - 3, B):
                second(b, b % 2)
            pool.wait_ge(rstd2_done, B)
            select_pairs(2)
            const(g.memset(pick_zero[:, :], 0.0))
            for part in range(3):
                const(g.affine_select(out=pick_zero[:, :], in_=pick_zero[:, :], compare_op=ALU.not_equal, fill=1.0,
                                      base=-(E_R + 1) * part - E_R, pattern=[[0, P]], channel_multiplier=1))
            assert made[0] == N_POOL_CONST, made[0]
            with pool.Fori(0, B) as b:
                pool.wait_ge(z2_done, b + 1)
                g.tensor_tensor(h_all[:, b, :, :], h_all[:, b, :, :], row(R_GA, b), ALU.mult).then_inc(res_chain, 1)
                pool.wait_ge(res_chain, b + 1)
                g.tensor_tensor(h_all[:, b, :, :], h_all[:, b, :, :], x_all[:, b, :, :], ALU.add).then_inc(res_done, 1)

            def prepare_x1(n):
                pool.wait_ge(v_done, n + 1)
                g.tensor_tensor(h_all[:, n, :, :], v_t[:, :, :], h_all[:, n, :, :], ALU.add).then_inc(x1_done, 1)

            def prepare_rstd(n):
                pool.wait_ge(pool_const, N_POOL_CONST)
                pool.wait_ge(stats3_done, n + 1)
                wait(pool, z_done, n)
                g.tensor_scalar_add(ve3[:, :], mv3[:, :, 1], EPS)
                g.tensor_scalar_mul(nm3[:, :], mv3[:, :, 0], -1.0).then_inc(nm3_done, 1)
                pool.wait_ge(nm3_done, n + 1)
                g.tensor_tensor(rs3[:, :], ve3[:, :], minus_half[:, :], ALU.pow).then_inc(pow3_done, 1)
                pool.wait_ge(pow3_done, n + 1)
                g.tensor_tensor(mr3[:, :], nm3[:, :], rs3[:, :], ALU.mult).then_inc(rstd3_done, 1)

            def prepare_lo(n, par):
                pool.wait_ge(h2_hi_done, n + 1)
                g.tensor_tensor(h2_lo[:, par, :], h2t[:, :], h2_hi[:, par, :].bitcast(F32), ALU.subtract).then_inc(h2_lo_done, 1)

            def experts(c, par, has_next):
                for p in range(PAIRS):
                    q = c * PAIRS + p
                    wait(pool, down_mm, q - 3)
                    pool.wait_ge(hi_done, q + 1)
                    g.tensor_tensor(act_lo[:, p % 4, :], act4[:, p % 4, :], act_hi[:, p % 4, :].bitcast(F32),
                                    ALU.subtract).then_inc(lo_done, 1)
                    if has_next and p == 0:
                        prepare_x1(c + 1)
                    if has_next and p == 2:
                        prepare_rstd(c + 1)
                    if has_next and p == 6:
                        prepare_lo(c + 1, 1 - par)

            pool.wait_ge(res_done, B)
            prepare_x1(0)
            prepare_rstd(0)
            prepare_lo(0, 0)
            experts(0, 0, True)
            with pool.Fori(0, (B - 2) // 2) as i:
                experts(i * 2 + 1, 1, True)
                experts(i * 2 + 2, 0, True)
            experts(B - 1, 1, False)

        @block.scalar
        def _(act):
            a = nc.scalar
            act.dma_start(c_row[:, :], cond).then_inc(in_cond, 16)
            act.dma_start(wmod_sb[:, :], wmod).then_inc(in_wmod, 16)
            act.dma_start(small[:, 0:S], A).then_inc(in_small, 16)
            act.dma_start(small[:, S:S + P], C).then_inc(in_small, 16)
            act.dma_start(small[:, S + P:S + P + 1], b_delta.unsqueeze(1)).then_inc(in_small, 16)
            act.dma_start(small[:, S + P + 1:S + P + 2], b_in.unsqueeze(1)).then_inc(in_small, 16)
            act.wait_ge(pool_const, 3)
            a.activation(warm[:, 0:1], minus_half[:, 0:1], ACT.Silu)
            act.wait_ge(in_cond, 16)
            a.activation(c_silu[:, :], c_row[:, :], ACT.Silu).then_inc(c_silu_done, 1)
            act.wait_ge(w_pad_done, 1)
            act.dma_start(w_pad[:, W_PAD:W_PAD + S], w_delta).then_inc(in_w, 16)
            act.dma_start(w_pad[:, W_PAD + S:W_PAD + 2 * S], w_in).then_inc(in_w, 16)
            a.activation(warm[:, 1:2], minus_half[:, 0:1], ACT.Sigmoid)

            def take_rows(k):
                act.wait_ge(rows_mm, k + 1)
                b0 = 4 * ROW_ORDER[k][2]
                a.activation(rows[:, ROW_ORDER[k][0], b0:b0 + 4, :].rearrange("p b d -> p (b d)"),
                             bank[:, ROWS_B[k], :], ACT.Identity).then_inc(rows_out, 1)

            def first(b, par):
                wait_apart(act, rstd1_done, b + 1)
                for j in range(NT):
                    done = a.activation(h_all[:, b, j, :], x_all[:, b, j, :], ACT.Identity,
                                        bias=mr[:, 0, par, j:j + 1], scale=rs[:, 0, par, j:j + 1])
                done.then_inc(z1_done, 1)

            def second(b, par):
                wait_apart(act, rstd2_done, b + 1)
                for j in range(NT):
                    done = a.activation(xn_all[:, b, j * P:(j + 1) * P], h_all[:, b, j, :], ACT.Identity,
                                        bias=mr[:, 1, par, j:j + 1], scale=rs[:, 1, par, j:j + 1])
                done.then_inc(z2_done, 1)

            def affine(b, par):
                wait_apart(act, z2t_done, b + 1)
                a.activation(xn_all[:, b, :], bank[:, MISC[par], :], ACT.Identity,
                             bias=gb_col[:, 1:2], scale=gb_col[:, 0:1]).then_inc(xnt_done, 1)

            first(0, 0)
            take_rows(0)
            take_rows(1)
            first(1, 1)
            take_rows(2)
            take_rows(3)
            first(2, 0)
            take_rows(4)
            take_rows(5)
            second(0, 0)
            act.wait_ge(in_affine, 32)
            first(3, 1)
            second(1, 1)
            affine(0, 0)
            with act.Fori(0, (B - 4) // 2) as i:
                first(i * 2 + 4, 0)
                second(i * 2 + 2, 0)
                affine(i * 2 + 1, 1)
                first(i * 2 + 5, 1)
                second(i * 2 + 3, 1)
                affine(i * 2 + 2, 0)
            second(B - 2, 0)
            affine(B - 3, 1)
            second(B - 1, 1)
            affine(B - 2, 0)
            affine(B - 1, 1)
            act.wait_ge(small_done, 1)
            for g in range(GROUPS):
                act.wait_ge(proj_done, g + 1)
                a.activation(delta[:, g * T:(g + 1) * T], bank[:, PROJ_B[g], :], ACT.Sigmoid,
                             bias=small_rep[:, S + P:S + P + 1]).then_inc(delta_out, 1)

            for n in range(SWEEP_STEPS):
                k = n % SEG_LEN
                act.wait_ge(step_mm, n + 1)
                a.activation(H[:, k::SEG_LEN], bank[:, SCAN[n % 2], 0:COLS], ACT.Tanh).then_inc(step_h, 1)
                if n < len(SIDE_WORK):
                    kind, m = SIDE_WORK[n]
                    act.wait_ge(side_mm, n + 1)
                    src = bank[:, SIDE[n % NS], :]
                    if kind == "weights":
                        a.activation(w_hi[:, m // 4, 4 * (m % 4):4 * (m % 4) + 4, :].rearrange("p k d -> p (k d)"),
                                     src, ACT.Identity).then_inc(side_hi, 1)
                    else:
                        half = 256 * (m % 2)
                        a.activation(xn_all[:, m // 2, half:half + 256], src[:, 0:256], ACT.Sigmoid).then_inc(side_gate, 1)
            a.activation(warm[:, 2:3], minus_half[:, 0:1], ACT.Exp)
            act.wait_ge(verdict, 1)
            go_on = act.value_load(again[0:1, 0:1])
            with act.If(go_on != 0):
                with act.Fori(0, SEGS - 2) as s:
                    with act.Fori(0, SEG_LEN) as k:
                        act.wait_ge(more_mm, s * SEG_LEN + k + 1)
                        a.activation(H[:, bass.ds(k, COLS, SEG_LEN)], bank[:, SCAN[0], 0:COLS], ACT.Tanh).then_inc(more_h, 1)

            def prepare_z(n):
                wait_apart(act, rstd3_done, n + 1)
                wait(act, zt_mm, n)
                for j in range(NT):
                    done = a.activation(z[:, j, :], h_all[:, n, j, :], ACT.Identity,
                                        bias=mr3[:, j:j + 1], scale=rs3[:, j:j + 1])
                done.then_inc(z_done, 1)

            def prepare_h2(n, par):
                act.wait_ge(zt_mm, n + 1)
                wait(act, h2_lo_done, n)
                wait(act, zero_done, n)
                a.activation(h2t[:, :], bank[:, PREP_B, :], ACT.Identity,
                             bias=now_mod[:, 0:1], scale=now_mod[:, 1:2]).then_inc(h2t_done, 1)
                act.wait_ge(h2t_done, n + 1)
                a.activation(h2_hi[:, par, :], h2t[:, :], ACT.Identity).then_inc(h2_hi_done, 1)

            def prepare_exp(n):
                act.wait_ge(shifted_done, n + 1)
                a.activation(ex[:, :, :], ls[:, :, :], ACT.Exp).then_inc(exp_done, 1)

            def prepare_w3t(n):
                act.wait_ge(w3t_mm, n + 1)
                wait(act, route_mm, n * PAIRS)
                a.activation(w3t[:, :], bank[0:W_ROWS, PREP_B, :].bitcast(BF16)[:, 0:512], ACT.Identity).then_inc(w3t_done, 1)

            def high_part(q, slot):
                wait(act, down_mm, q - 3)
                act.wait_ge(act_done, q + 1)
                a.activation(act_hi[:, slot, :], act4[:, slot, :], ACT.Identity).then_inc(hi_done, 1)

            def experts(c, par, has_prev, has_next):
                for p in range(PAIRS):
                    q = c * PAIRS + p
                    if p == 0:
                        prepare_w3t(c)
                    wait(act, gated_done, q - 1)
                    act.wait_ge(gate_mm, q + 1)
                    a.activation(silu_g[:, p % 2, :], bank[:, GATE_B[p % 2], :], ACT.Silu).then_inc(silu_done, 1)
                    if has_next and p == 9:
                        prepare_exp(c + 1)
                    if p > 0 or has_prev:
                        high_part(q - 1, (p - 1) % 4)
                    if has_next and p == 4:
                        prepare_z(c + 1)
                    if has_next and p == 6:
                        prepare_h2(c + 1, 1 - par)

            prepare_z(0)
            prepare_h2(0, 0)
            prepare_exp(0)
            experts(0, 0, False, True)
            with act.Fori(0, (B - 2) // 2) as i:
                experts(i * 2 + 1, 1, True, True)
                experts(i * 2 + 2, 0, True, True)
            experts(B - 1, 1, True, False)
            high_part(B * PAIRS - 1, (PAIRS - 1) % 4)

        @block.vector
        def _(dve):
            v = nc.vector
            chained = [0]

            def chain(ins):
                chained[0] += 1
                ins.then_inc(dve_chain, 1)
                dve.wait_ge(dve_chain, chained[0])

            v.memset(ones_col[:, :], 1.0)
            v.memset(a_block[:, :, :, :], 0.0)
            v.memset(w_pad[:, :], 0.0).then_inc(w_pad_done, 1)

            def spread(source, to, done):
                for j in range(NT):
                    last = v.bn_stats(to[:, j, :], source(j))
                last.then_inc(done, 1)

            def moments(norm, par, source, done):
                for j in range(NT):
                    last = v.bn_aggr(mv[:, norm, par, j, :], source[:, par, j, :])
                last.then_inc(done, 1)

            dve.wait_ge(ct_mm, 1)
            v.tensor_copy(c_silu_t[:, :], bank[:, SETUP_B, 0:B]).then_inc(ct_done, 1)
            dve.wait_ge(in_x, 16 * 4)
            spread(lambda j: x_all[:, 0, j, :], stats1[:, 0], spread1)
            dve.wait_ge(spread1, 1)
            moments(0, 0, stats1, moments1)
            dve.wait_ge(mod_mm, 1)
            raw = bank[:, SETUP_B, 0:NMOD * B].rearrange("p (m b) -> p m b", m=NMOD)
            chain(v.tensor_copy(modt[:, :, :], raw))
            v.tensor_scalar_add(modt[:, CB1, :], modt[:, CB1, :], 1.0)
            v.tensor_scalar_add(modt[:, CA1, :], modt[:, CA1, :], 1.0).then_inc(scale_done, 1)
            spread(lambda j: x_all[:, 1, j, :], stats1[:, 1], spread1)
            dve.wait_ge(spread1, 2)
            moments(0, 1, stats1, moments1)
            both = modt[:, GA:GB + 1:GB - GA, :]
            chain(v.tensor_scalar(mod_tmp[:, 0, :, :], both, 0.0, 2.0, ALU.is_ge, ALU.mult))
            chain(v.tensor_scalar_add(mod_tmp[:, 0, :, :], mod_tmp[:, 0, :, :], -1.0))
            chain(v.tensor_tensor(mod_tmp[:, 1, :, :], both, mod_tmp[:, 0, :, :], ALU.mult))
            chain(v.scalar_tensor_tensor(out=both, in0=mod_tmp[:, 1, :, :], scalar=MOD_FLOOR,
                                         in1=mod_tmp[:, 0, :, :], op0=ALU.max, op1=ALU.mult))
            v.tensor_copy(ga_rep[:, :, :, :], modt[:, GA, :].rearrange("p (b4 g) -> p g b4", g=GROUPS).unsqueeze(3)
                          .broadcast_to([P, GROUPS, BG, 2 * S])).then_inc(ga_done, 1)

            def scale(b, par, has_last):
                if has_last:
                    dve.wait_ge(spread2, b)
                dve.wait_ge(z1_done, b + 1)
                v.tensor_tensor(h_all[:, b, :, :], h_all[:, b, :, :], row(R_CA1, b), ALU.mult).then_inc(h_chain, 1)
                if has_last:
                    moments(1, 1 - par, stats2, moments2)

            def shift(b, par, has_ahead):
                if has_ahead:
                    dve.wait_ge(spread1, b + 3)
                dve.wait_ge(h_chain, b + 1)
                v.tensor_tensor(h_all[:, b, :, :], h_all[:, b, :, :], row(R_SA, b), ALU.add).then_inc(h_done, 1)
                if has_ahead:
                    moments(0, par, stats1, moments1)

            def spread_h(b, par):
                dve.wait_ge(in_x, 16 * 4)
                dve.wait_ge(h_done, b + 1)
                spread(lambda j: h_all[:, b, j, :], stats2[:, par], spread2)

            def step(b, par, has_last, has_ahead):
                scale(b, par, has_last)
                if has_ahead:
                    spread(lambda j: x_all[:, b + 2, j, :], stats1[:, par], spread1)
                shift(b, par, has_ahead)
                spread_h(b, par)

            dve.wait_ge(rows_out, 2)
            step(0, 0, False, True)
            step(1, 1, True, True)
            dve.wait_ge(rows_out, 4)
            with dve.Fori(0, (B - 4) // 2) as i:
                step(i * 2 + 2, 0, True, True)
                step(i * 2 + 3, 1, True, True)
            step(B - 2, 0, True, False)
            step(B - 1, 1, True, False)
            dve.wait_ge(spread2, B)
            dve.wait_ge(rstd2_done, B - 2)
            moments(1, 1, stats2, moments2)

            dve.wait_ge(ga_rep_mm, 1)
            v.tensor_copy(small_rep[:, :], bank[:, SETUP_B, AT_SMALL:AT_SMALL + S + P + 1]).then_inc(small_done, 1)
            chain(v.tensor_copy(cls_t[:, :], bank[:, SETUP_B, AT_CLS:AT_CLS + E_T]))
            v.tensor_tensor(a_block[:, :, 0, :], small_rep[:, 0:S].unsqueeze(1).broadcast_to([P, BG, S]),
                            own_batch[:, :].unsqueeze(2).broadcast_to([P, BG, S]), ALU.mult)
            chain(v.tensor_tensor(c_ga[:, :, :], bank[:, SETUP_B, AT_GA:AT_GA + GROUPS * P].rearrange("p (g d) -> p g d", g=GROUPS),
                                  small_rep[:, S:S + P].unsqueeze(1).broadcast_to([P, GROUPS, P]), ALU.mult))
            v.tensor_tensor(c_batch[:, :, :].rearrange("p (b4 g) d -> p b4 g d", g=GROUPS),
                            c_ga[:, :, :].unsqueeze(1).broadcast_to([P, BG, GROUPS, P]),
                            own_batch[:, :].unsqueeze(2).unsqueeze(3).broadcast_to([P, BG, GROUPS, P]),
                            ALU.mult)
            dve.wait_ge(in_late, 64)
            chain(v.tensor_copy(bg_part[:, 0, :], bg3[:, :]))
            chain(v.tensor_tensor(bg_rest[:, 0, :], bg3[:, :], bg_part[:, 0, :], ALU.subtract))
            chain(v.tensor_copy(bg_part[:, 1, :], bg_rest[:, 0, :]))
            chain(v.tensor_tensor(bg_rest[:, 1, :], bg_rest[:, 0, :], bg_part[:, 1, :], ALU.subtract))
            chain(v.tensor_copy(bg_part[:, 2, :], bg_rest[:, 1, :]))
            chain(v.tensor_scalar_mul(bg_mix[:, :], bg_part[:, 0, :], ident[0:3, 0:1]))
            chain(v.scalar_tensor_tensor(out=bg_mix[:, :], in0=bg_part[:, 1, :], scalar=ident[0:3, 1:2], in1=bg_mix[:, :],
                                         op0=ALU.mult, op1=ALU.add))
            v.scalar_tensor_tensor(out=bg_rows[:, :], in0=bg_part[:, 2, :], scalar=ident[0:3, 2:3], in1=bg_mix[:, :],
                                   op0=ALU.mult, op1=ALU.add).then_inc(bg_done, 1)
            for g in range(GROUPS):
                dve.wait_ge(delta_out, g + 1)
                v.tensor_scalar(drive[:, g * T:(g + 1) * T], bank[:, PROJ_B[g], :], small_rep[:, S + P:S + P + 1],
                                None, ALU.add).then_inc(drive_out, 1)

            H3 = H[:, :].rearrange("p (g t) -> p g t", g=GROUPS)
            delta3 = delta[:, :].rearrange("p (g t) -> p g t", g=GROUPS)

            def first_in(to):
                return v.tensor_tensor(to[:, :].rearrange("p (g c) -> p g c", g=GROUPS)[:, :, 1:SEGS],
                                       H3[:, :, SEG_LEN - 1:T - SEG_LEN:SEG_LEN], delta3[:, :, SEG_LEN::SEG_LEN], ALU.mult)

            dve.wait_ge(delta_out, GROUPS)
            for n in range(SWEEP_STEPS):
                k = n % SEG_LEN
                dve.wait_ge(step_h, n + 1)
                if k < SEG_LEN - 1:
                    v.tensor_tensor(h_in[:, :], H[:, k::SEG_LEN], delta[:, k + 1::SEG_LEN], ALU.mult).then_inc(step_in, 1)
                elif n < SWEEP_STEPS - 1:
                    first_in(h_in0).then_inc(step_in, 1)
                    v.tensor_copy(ends[:, :], H[:, k::SEG_LEN])
                else:
                    chain(v.tensor_tensor(differ[:, :], H[:, k::SEG_LEN], ends[:, :], ALU.not_equal))
                    v.tensor_reduce(differ_p[:, :], differ[:, :], AX, ALU.max).then_inc(step_in, 1)
                if n < len(SIDE_WORK) and SIDE_WORK[n][0] == "weights":
                    m = SIDE_WORK[n][1]
                    dve.wait_ge(side_hi, m + 1)
                    part = (slice(None), m // 4, slice(4 * (m % 4), 4 * (m % 4) + 4), slice(None))
                    v.tensor_tensor(w_lo[part].rearrange("p k d -> p (k d)"), bank[:, SIDE[n % NS], :],
                                    w_hi[part].rearrange("p k d -> p (k d)").bitcast(F32), ALU.subtract).then_inc(side_lo, 1)
            dve.wait_ge(verdict_mm, 1)
            v.tensor_copy(again[:, :], bank[0:1, SCAN[0], 0:1]).then_inc(verdict, 1)
            dve.wait_ge(verdict, 1)
            go_on = dve.value_load(again[0:1, 0:1])
            with dve.If(go_on != 0):
                with dve.Fori(0, SEGS - 2) as s:
                    first_in(h_in)
                    v.memset(h_in[:, 0:COLS:SEGS], 0.0).then_inc(more_in, 1)
                    with dve.Fori(0, SEG_LEN - 1) as k:
                        dve.wait_ge(more_h, s * SEG_LEN + k + 1)
                        v.tensor_tensor(h_in[:, :], H[:, bass.ds(k, COLS, SEG_LEN)], delta[:, bass.ds(k + 1, COLS, SEG_LEN)],
                                        ALU.mult).then_inc(more_in, 1)
                    dve.wait_ge(more_h, s * SEG_LEN + SEG_LEN)

            PRE = 17
            at = [0]

            def mark(ins):
                at[0] += 1
                ins.then_inc(pre_chain, 1)

            def after(n):
                dve.wait_ge(pre_chain, n * PRE + at[0])

            def prepare_v(n):
                dve.wait_ge(y_mm, n + 1)
                wait(dve, x1_done, n)
                v.tensor_tensor(v_t[:, :, :].rearrange("p j d -> p (j d)"), bank[:, PREP_B, :], xn_all[:, n, :],
                                ALU.mult).then_inc(v_done, 1)

            def prepare_stats(n):
                dve.wait_ge(in_x, 16 * 4)
                dve.wait_ge(x1_done, n + 1)
                for j in range(NT):
                    last = v.bn_stats(stats[:, j, :], h_all[:, n, j, :])
                last.then_inc(var3_done, 1)

            def prepare_moments(n):
                dve.wait_ge(in_x, 16 * 4)
                dve.wait_ge(var3_done, n + 1)
                wait(dve, rstd3_done, n)
                for j in range(NT):
                    last = v.bn_aggr(mv3[:, j, :], stats[:, j, :])
                    if j == 0:
                        v.tensor_copy(now_mod[:, :], modt[:, SB_:CB1 + 1, n])
                last.then_inc(stats3_done, 1)

            def over(t):
                return t.unsqueeze(2).broadcast_to([P, NT, E_T])

            def prepare_shift(n):
                dve.wait_ge(logit_mm, n + 1)
                logits = bank[:, PREP_B, 0:NT * E_T].rearrange("p (j e) -> p j e", j=NT)
                mark(v.tensor_reduce(lmax[:, :], logits, AX, ALU.max))
                after(n)
                v.tensor_tensor(ls[:, :, :], logits, over(lmax[:, :]), ALU.subtract).then_inc(shifted_done, 1)

            def prepare_sum(n):
                dve.wait_ge(exp_done, n + 1)
                mark(v.tensor_reduce(esum[:, :], ex[:, :, :], AX, ALU.add))
                after(n)
                mark(v.reciprocal(erec[:, :], esum[:, :]))

            def prepare_scores(n):
                after(n)
                mark(v.tensor_tensor(score[:, :, :], ex[:, :, :], over(erec[:, :]), ALU.mult))
                after(n)
                mark(v.tensor_tensor(biased[:, :, :], score[:, :, :],
                                     route_bias_sb[:, :].unsqueeze(1).broadcast_to([P, NT, E_T]), ALU.add))

            def prepare_top(n):
                after(n)
                v.tensor_scalar_mul(scaled[:, :, :], score[:, :, :], ROUTE_SCALE)
                for j in range(NT):
                    last = v.max(top8[:, j, :], biased[:, j, :])
                mark(last)

            def prepare_place(n):
                after(n)
                v.tensor_tensor(at_or_above[:, :, :], biased[:, :, :], over(top8[:, :, TOP_K - 1]), ALU.is_ge)
                for j in range(NT):
                    last = v.max_index(top8_at[:, j, :], top8[:, j, :], biased[:, j, :])
                mark(last)

            def prepare_above(n):
                v.tensor_tensor(above[:, :, :], biased[:, :, :], over(top8[:, :, TOP_K - 1]), ALU.is_gt)
                after(n)
                mark(v.tensor_copy(last_at[:, :], top8_at[:, :, TOP_K - 1]))
                after(n)
                mark(v.tensor_tensor(early[:, :, :], expert_no[:, :].unsqueeze(1).broadcast_to([P, NT, E_T]),
                                     over(last_at[:, :]), ALU.is_le))

            def prepare_chosen(n):
                after(n)
                mark(v.tensor_tensor(above[:, :, :], above[:, :, :], early[:, :, :], ALU.max))
                after(n)
                mark(v.tensor_tensor(above[:, :, :], above[:, :, :], at_or_above[:, :, :], ALU.mult))

            def prepare_weights(n):
                after(n)
                mark(v.tensor_tensor(weight[:, :, :], above[:, :, :], scaled[:, :, :], ALU.mult))
                after(n)
                mark(v.tensor_reduce(zero_w[:, :], weight[:, :, E_R:E_T], AX, ALU.add))

            def prepare_part1(n):
                after(n)
                mark(v.tensor_copy(weight[:, :, E_R], zero_w[:, :]))
                after(n)
                mark(v.tensor_copy(w3[:, :, 0, :], weight[:, :, 0:E_R + 1]))

            def prepare_part2(n):
                after(n)
                mark(v.tensor_tensor(rest1[:, :, :], weight[:, :, 0:E_R + 1], w3[:, :, 0, :], ALU.subtract))
                after(n)
                mark(v.tensor_copy(w3[:, :, 1, :], rest1[:, :, :]))

            def prepare_part3(n):
                after(n)
                v.tensor_tensor(w3[:, :, 2, :], rest1[:, :, :], w3[:, :, 1, :], ALU.subtract).then_inc(w3_done, 1)
                assert at[0] == PRE, at[0]

            def zero_experts(c, par):
                wait(dve, f_done, c - 1)
                v.tensor_scalar_mul(now_gb[:, par:par + 1], modt[:, GB, bass.ds(c, 1)], 1.0).then_inc(gb_ready, 1)
                dve.wait_ge(zero_mm, c + 1)
                dve.wait_ge(gb_ready, c + 1)
                v.scalar_tensor_tensor(out=zero_part[:, par, :], in0=h2t[:, :], scalar=now_gb[:, par:par + 1],
                                       in1=bank[:, PREP_B, :], op0=ALU.mult, op1=ALU.mult).then_inc(zero_done, 1)

            def leave_down(c, par):
                dve.wait_ge(down_mm, (c + 1) * PAIRS)
                dve.wait_ge(zero_done, c + 1)
                wait(dve, ft_mm, c)
                v.scalar_tensor_tensor(out=f_t[:, :], in0=bank[:, DOWN_B, :], scalar=now_gb[:, par:par + 1],
                                       in1=zero_part[:, par, :], op0=ALU.mult, op1=ALU.add).then_inc(f_done, 1)

            def finish(c):
                dve.wait_ge(ft_mm, c + 1)
                wait(dve, out_dma, 16 * c)
                v.tensor_tensor(out_sb[:, :, :].rearrange("p j d -> p (j d)"), bank[:, PREP_B, :],
                                h_all[:, c, :, :].rearrange("p j d -> p (j d)"), ALU.add).then_inc(out_ready, 1)

            def experts(c, par, has_prev, has_next):
                for p in range(PAIRS):
                    q = c * PAIRS + p
                    if has_prev and p == 3:
                        leave_down(c - 1, 1 - par)
                    dve.wait_ge(silu_done, q + 1)
                    dve.wait_ge(up_mm, q + 1)
                    wait(dve, act_done, q - 1)
                    v.tensor_tensor(gated[:, p % 2, :], silu_g[:, p % 2, :], bank[:, UP_B[p % 2], :], ALU.mult).then_inc(gated_done, 1)
                    if has_next and p == 0:
                        prepare_v(c + 1)
                    if p == 1:
                        zero_experts(c, par)
                    if has_next and p == 2:
                        prepare_stats(c + 1)
                    if has_next and p == 3:
                        prepare_moments(c + 1)
                    if has_next and p == 8:
                        at[0] = 0
                        prepare_shift(c + 1)
                    if has_next and p == 10:
                        prepare_sum(c + 1)
                    if has_next and p == 11:
                        prepare_top(c + 1)
                    if has_next and p == 12:
                        prepare_above(c + 1)
                    if has_next and p == 13:
                        prepare_weights(c + 1)
                    if has_next and p == 14:
                        prepare_part2(c + 1)
                    dve.wait_ge(gated_done, q + 1)
                    dve.wait_ge(route_mm, q + 1)
                    wait(dve, lo_done, q - 3)
                    v.tensor_tensor(act4[:, p % 4, :], gated[:, p % 2, :], bank[:, ROUTE_B[p % 2], :], ALU.mult).then_inc(act_done, 1)
                    if has_prev and p == 4:
                        finish(c - 1)
                    if has_next and p == 10:
                        prepare_scores(c + 1)
                    if has_next and p == 11:
                        prepare_place(c + 1)
                    if has_next and p == 12:
                        prepare_chosen(c + 1)
                    if has_next and p == 13:
                        prepare_part1(c + 1)
                    if has_next and p == 14:
                        prepare_part3(c + 1)

            dve.wait_ge(side_gate, N_GATES)
            prepare_v(0)
            prepare_stats(0)
            prepare_moments(0)
            prepare_shift(0)
            prepare_sum(0)
            prepare_scores(0)
            prepare_top(0)
            prepare_place(0)
            prepare_above(0)
            prepare_chosen(0)
            prepare_weights(0)
            prepare_part1(0)
            prepare_part2(0)
            prepare_part3(0)
            experts(0, 0, False, True)
            with dve.Fori(0, (B - 2) // 2) as i:
                experts(i * 2 + 1, 1, True, True)
                experts(i * 2 + 2, 0, True, True)
            experts(B - 1, 1, True, False)
            leave_down(B - 1, 1)
            finish(B - 1)

        @block.tensor
        def _(pe):
            mm = nc.tensor.matmul
            pe.wait_ge(pool_const, N_SETUP_CONST)
            pe.wait_ge(c_silu_done, 1)
            nc.tensor.transpose(bank[:, SETUP_B, 0:B], c_silu[:, :], ident[0:B, 0:B]).then_inc(ct_mm, 1)
            pe.wait_ge(ct_done, 1)
            pe.wait_ge(in_wmod, 16)
            for m in range(NMOD):
                done = mm(bank[:, SETUP_B, m * B:(m + 1) * B], wmod_sb[:, m * P:(m + 1) * P], c_silu_t[:, :], start=True, stop=True)
            done.then_inc(mod_mm, 1)
            pe.wait_ge(scale_done, 1)

            def broadcast_row(dst, k, b):
                return mm(dst, modt[:, k, b:b + 1].broadcast_to([P, P]), ident[:, 0:P], start=True, stop=True)

            for k in range(6):
                if k == 4:
                    pe.wait_ge(ga_done, 1)
                for r in range(4):
                    done = broadcast_row(bank[:, ROWS_B[k], r * P:(r + 1) * P], ROW_ORDER[k][1], 4 * ROW_ORDER[k][2] + r)
                done.then_inc(rows_mm, 1)
            for g in range(GROUPS):
                mm(bank[:, SETUP_B, AT_GA + g * P:AT_GA + (g + 1) * P], ga_rep[:, g, :, :].rearrange("d b s -> d (b s)"), ident[:, 0:P],
                   start=True, stop=True)
            pe.wait_ge(in_small, 64)
            pe.wait_ge(in_late, 64)
            mm(bank[:, SETUP_B, AT_SMALL:AT_SMALL + S + P + 1], spread_rows[:, 0, :, :, :].rearrange("k b w s -> k (b w s)"),
               small[:, 0:S + P + 1], start=True, stop=True)
            mm(bank[:, SETUP_B, AT_SMALL + S + P:AT_SMALL + S + P + 1], spread_rows[:, 1, :, :, :].rearrange("k b w s -> k (b w s)"),
               small[:, S + P + 1:S + P + 2], start=False, stop=True, skip_group_check=True)
            nc.tensor.transpose(bank[:, SETUP_B, AT_CLS:AT_CLS + E_T], cls_sb[:, :], ident[0:E_T, 0:E_T]).then_inc(ga_rep_mm, 1)

            pe.wait_ge(rows_out, 6)
            pe.wait_ge(in_w, 32)

            def project(b):
                pe.wait_ge(xnt_done, b + 1)
                b4, g = b // GROUPS, b % GROUPS
                lo = W_PAD - 2 * S * b4
                done = mm(bank[:, PROJ_B[g], :], w_pad[:, lo:lo + P], xn_all[:, b, :], start=b4 == 0, stop=b4 == BG - 1)
                if b4 == BG - 1:
                    done.then_inc(proj_done, 1)

            for b in range(B):
                pe.wait_ge(z2_done, b + 1)
                wait(pe, xnt_done, b - 1)
                for j in range(NT):
                    done = nc.tensor.transpose(bank[:, MISC[b % 2], j * P:(j + 1) * P], xn_all[:, b, j * P:(j + 1) * P], ident[:, 0:P])
                done.then_inc(z2t_done, 1)
                if b:
                    project(b - 1)
            project(B - 1)
            def seed(dst, cols, last):
                return mm(dst, ident[:, S:S + P], drive[:, cols], start=True, stop=last)

            def side(n):
                kind, m = SIDE_WORK[n]
                to = bank[:, SIDE[n % NS], :]
                if n >= NS:
                    pe.wait_ge(*side_read(n - NS))
                if kind == "weights":
                    which, g = m // 4, m % 4
                    pe.wait_ge(in_dn if which == 2 else in_gu, 16 if which == 2 else 64)
                    for r in range(4):
                        pair = 4 * g + r
                        src = (dn_raw[:, 2 * pair:2 * pair + 2, :].rearrange("h e i -> h (e i)") if which == 2
                               else gu_raw[:, which, pair, :])
                        done = nc.tensor.transpose(to[:, r * P:(r + 1) * P], src, ident[:, 0:P])
                else:
                    b, half = m // 2, m % 2
                    mm(to[:, 0:256], ones3[:, :], bg_rows[:, :].unsqueeze(1).broadcast_to([3, 2, P]), start=True, stop=True)
                    for j in range(2):
                        j0 = (2 * half + j) * P
                        done = mm(to[:, j * P:(j + 1) * P], xn_all[:, b, j0:j0 + P], wg_sb[:, :],
                                  start=False, stop=True, skip_group_check=True)
                done.then_inc(side_mm, 1)

            pe.wait_ge(bg_done, 1)
            pe.wait_ge(drive_out, GROUPS)
            pe.wait_ge(delta_out, GROUPS)
            a_all = a_block[:, :, :, :].rearrange("p b w s -> p (b w s)")
            seed(bank[:, SCAN[0], 0:COLS], slice(0, None, SEG_LEN), True).then_inc(step_mm, 1)
            for n in range(1, SWEEP_STEPS):
                k = n % SEG_LEN
                dst = bank[:, SCAN[n % 2], 0:COLS]
                seed(dst, slice(k, None, SEG_LEN), False)
                if n - 1 < len(SIDE_WORK):
                    side(n - 1)
                pe.wait_ge(step_in, n)
                mm(dst, a_all, (h_in if k else h_in0)[:, :], start=False, stop=True).then_inc(step_mm, 1)
            pe.wait_ge(step_in, SWEEP_STEPS)
            mm(bank[0:1, SCAN[0], 0:1], differ_p[:, :], ones_col[:, :], start=True, stop=True).then_inc(verdict_mm, 1)
            pe.wait_ge(verdict, 1)
            go_on = pe.value_load(again[0:1, 0:1])
            with pe.If(go_on != 0):
                with pe.Fori(0, SEGS - 2) as s:
                    with pe.Fori(0, SEG_LEN) as k:
                        pe.wait_ge(more_in, s * SEG_LEN + k + 1)
                        seed(bank[:, SCAN[0], 0:COLS], bass.ds(k, COLS, SEG_LEN), False)
                        mm(bank[:, SCAN[0], 0:COLS], a_all, h_in[:, :],
                           start=False, stop=True).then_inc(more_mm, 1)
                pe.wait_ge(more_h, (SEGS - 2) * SEG_LEN)

            def prepare_y(n, g):
                wait(pe, w3t_done, n)
                for j in range(NT):
                    done = mm(bank[:, PREP_B, j * P:(j + 1) * P], H[:, g * T + j * P:g * T + (j + 1) * P], c_batch[:, n, :], start=True, stop=True)
                done.then_inc(y_mm, 1)

            def prepare_zt(n):
                pe.wait_ge(z_done, n + 1)
                wait(pe, zero_done, n)
                wait(pe, out_ready, n - 1)
                for j in range(NT):
                    done = nc.tensor.transpose(bank[:, PREP_B, j * P:(j + 1) * P], z[:, j, :], ident[:, 0:P])
                done.then_inc(zt_mm, 1)

            def prepare_logits(n):
                pe.wait_ge(h2t_done, n + 1)
                for j in range(NT):
                    done = mm(bank[:, PREP_B, j * E_T:(j + 1) * E_T], h2t[:, j * P:(j + 1) * P], cls_t[:, :], start=True, stop=True)
                done.then_inc(logit_mm, 1)

            def prepare_w3t(n):
                pe.wait_ge(w3_done, n + 1)
                to = bank[0:W_ROWS, PREP_B, :].bitcast(BF16)
                for j in range(NT):
                    done = nc.tensor.transpose(to[:, j * P:(j + 1) * P], w3[:, j, :, :].rearrange("p k e -> p (k e)"), ident_bf[:, :])
                done.then_inc(w3t_mm, 1)

            def split_product(dst, which, pair, hi, lo, first=True, last=True):
                mm(dst, w_hi[:, which, pair, :], hi, start=first, stop=False)
                mm(dst, w_hi[:, which, pair, :], lo, start=False, stop=False)
                return mm(dst, w_lo[:, which, pair, :], hi, start=False, stop=last)

            LAG = 3

            def down_product(c, p):
                q = c * PAIRS + p
                if p == 0:
                    wait(pe, f_done, c)
                pe.wait_ge(lo_done, q + 1)
                pe.wait_ge(hi_done, q + 1)
                split_product(bank[:, DOWN_B, :], 2, p, act_hi[:, p % 4, :], act_lo[:, p % 4, :],
                              p == 0, p == PAIRS - 1).then_inc(down_mm, 1)

            def zero_product(c, has_next):
                if has_next:
                    pe.wait_ge(v_done, c + 2)
                mm(bank[:, PREP_B, :], pick_zero[:, :], w3t[:, :], start=True, stop=True).then_inc(zero_mm, 1)

            def transpose_down(c):
                pe.wait_ge(f_done, c + 1)
                wait(pe, zero_done, min(c + 2, B) if isinstance(c, int) else c + 2)
                for j in range(NT):
                    done = nc.tensor.transpose(bank[:, PREP_B, j * P:(j + 1) * P], f_t[:, j * P:(j + 1) * P], ident[:, 0:P])
                done.then_inc(ft_mm, 1)

            def experts(c, par, has_prev, has_next):
                for p in range(PAIRS):
                    q = c * PAIRS + p
                    if p == 0:
                        pe.wait_ge(h2_lo_done, c + 1)
                    wait(pe, silu_done, q - 1)
                    split_product(bank[:, GATE_B[p % 2], :], 0, p, h2_hi[:, par, :], h2_lo[:, par, :]).then_inc(gate_mm, 1)
                    wait(pe, gated_done, q - 1)
                    split_product(bank[:, UP_B[p % 2], :], 1, p, h2_hi[:, par, :], h2_lo[:, par, :]).then_inc(up_mm, 1)
                    if has_next and p == 6:
                        prepare_zt(c + 1)
                    if p == 0:
                        prepare_w3t(c)
                        if has_prev:
                            down_product(c - 1, PAIRS - LAG)
                        pe.wait_ge(w3t_done, c + 1)
                    wait(pe, act_done, q - 1)
                    mm(bank[:, ROUTE_B[p % 2], :], pick_pair[:, p, :], w3t[:, :], start=True, stop=True).then_inc(route_mm, 1)
                    if has_prev and p == 4:
                        transpose_down(c - 1)
                    if p == LAG + 1:
                        down_product(c, 0)
                    if p > LAG:
                        down_product(c, p - LAG)
                    elif has_prev and 0 < p < LAG:
                        down_product(c - 1, PAIRS - LAG + p)
                    if has_next and p == 0:
                        prepare_y(c + 1, 1 - par)
                    if p == 1:
                        zero_product(c, has_next)
                    if has_next and p == 7:
                        prepare_logits(c + 1)

            pe.wait_ge(pool_const, N_POOL_CONST)
            pe.wait_ge(side_lo, N_WEIGHTS)
            pe.wait_ge(side_gate, N_GATES)
            prepare_y(0, 0)
            prepare_zt(0)
            prepare_logits(0)
            experts(0, 0, False, True)
            with pe.Fori(0, (B - 2) // 2) as i:
                experts(i * 2 + 1, 1, True, True)
                experts(i * 2 + 2, 0, True, True)
            experts(B - 1, 1, True, False)
            for p in range(PAIRS - LAG, PAIRS):
                down_product(B - 1, p)
            transpose_down(B - 1)


_INS = ['L0_attn_x', 'L0_attn_ln_gamma', 'L0_attn_ln_beta', 'L0_attn_A', 'L0_attn_C', 'L0_attn_w_delta',
        'L0_attn_b_delta', 'L0_attn_w_in', 'L0_attn_b_in', 'L0_attn_w_gate', 'L0_attn_b_gate',
        'L0_ffn_classifier_weight', 'L0_ffn_e_score_correction_bias', 'L0_ffn_gate_up_proj', 'L0_ffn_down_proj',
        'L0_c', 'L0_wmod']


def kernel(**inputs):
    import numpy as _np
    import concourse.bacc as _bacc
    from concourse import mybir as _mybir
    from concourse.bass_utils import run_bass_kernel_spmd as _run

    nc = _bacc.Bacc("TRN2", target_bir_lowering=False, num_devices=1)
    arrays, args = {}, []
    for name in _INS:
        a = _np.ascontiguousarray(inputs[name])
        arrays[f"in_{name}_dram"] = a
        args.append(nc.dram_tensor(f"in_{name}_dram", a.shape, _mybir.dt.from_np(a.dtype), kind="ExternalInput").ap())
    shape = inputs['L0_attn_x'].shape
    args.append(nc.dram_tensor("out_0_dram", shape, F32, kind="ExternalOutput").ap())
    adaln_block(nc, *args)
    r = _run(nc, [arrays], core_ids=[0])
    return r.results[0]["out_0_dram"]
```

```python
from contextlib import ExitStack

import concourse.bass as bass
from concourse import mybir

F32 = mybir.dt.float32
F32R = mybir.dt.float32r
BF16 = mybir.dt.bfloat16
I32 = mybir.dt.int32
ALU = mybir.AluOpType
ACT = mybir.ActivationFunctionType
AX = mybir.AxisListType.X

P = 128
EPS = 1e-5
TOP_K = 6
ROUTE_SCALE = 2.5
MOD_FLOOR = 0.25


def adaln_block(nc, x, ln_gamma, ln_beta, A, C, w_delta, b_delta, w_in, b_in, w_gate, b_gate,
                classifier, route_bias, gate_up, down, cond, wmod, out):
    B, T, D = x.shape
    S = A.shape[0]
    NT = T // P
    SEG_LEN = 16
    SEGS = T // SEG_LEN
    E_T = classifier.shape[0]
    E_R = down.shape[0]
    INNER = down.shape[2]
    GROUPS = 2
    BG = B // GROUPS
    PAIRS = E_R // 2
    NMOD = wmod.shape[1] // D
    assert D == P and BG * 2 * S == P and 2 * INNER == P and NT * P == 512 and gate_up.shape[1] == 2 * INNER

    with ExitStack() as ctx:
        def sb(name, shape, dt=F32):
            return ctx.enter_context(nc.sbuf_tensor(name, shape, dt))

        def sem(name):
            return ctx.enter_context(nc.semaphore(name))

        bank = ctx.enter_context(nc.psum_tensor("bank", [P, 8, 512], F32))
        SCAN = (0, 1)
        SIDE = (2, 3, 4, 5, 6, 7)
        GATE_B, UP_B = (0, 1), (2, 3)
        ROUTE_B = (4, 5)
        DOWN_B = 6
        PREP_B = 7
        MISC = (6, 7)
        PROJ_B = (0, 1)
        SETUP_B = 2
        AT_SMALL, AT_GA, AT_CLS = 64, 64 + S + P + 1, 64 + S + P + 1 + 2 * P
        ROWS_B = (3, 4, 5, 6, 7, 1)

        ident = sb("ident", [P, P + S])
        ones3 = sb("ones3", [3, P], BF16)
        own_batch = sb("own_batch", [P, BG])
        spread_rows = sb("spread_rows", [S, 2, BG, 2, S])
        minus_half = sb("minus_half", [P, NT])
        minus_one = sb("minus_one", [P, NT])
        eps = sb("eps", [P, NT])
        warm = sb("warm", [P, 3])
        W_ROWS = 3 * (E_R + 1)
        pick_pair = sb("pick_pair", [W_ROWS, PAIRS, P], BF16)
        pick_zero = sb("pick_zero", [W_ROWS, P], BF16)
        ident_bf = sb("ident_bf", [P, P], BF16)
        zero_bf = sb("zero_bf", [P, P], BF16)
        c_row = sb("c_row", [B, P])
        c_silu = sb("c_silu", [B, P])
        c_silu_t = sb("c_silu_t", [P, B])
        wmod_sb = sb("wmod_sb", [P, NMOD * P])
        SA, CA1, GA, SB_, CB1, GB = range(6)
        modt = sb("modt", [P, NMOD, B])
        mod_tmp = sb("mod_tmp", [P, 2, 2, B])
        R_SA, R_CA1, R_GA = range(3)
        rows = sb("rows", [P, 3, B, P])

        small = sb("small", [S, S + P + 2])
        small_rep = sb("small_rep", [P, S + P + 1])
        a_block = sb("a_block", [P, BG, 2, S])
        c_ga = sb("c_ga", [P, GROUPS, P])
        ga_rep = sb("ga_rep", [P, GROUPS, BG, 2 * S])
        c_batch = sb("c_batch", [P, B, P])
        W_PAD = P - 2 * S
        w_pad = sb("w_pad", [P, 2 * W_PAD + 2 * S])
        gb_col = sb("gb_col", [P, 2])
        wg_sb = sb("wg_sb", [P, P])
        bg3 = sb("bg3", [3, P])
        bg_part = sb("bg_part", [3, 3, P], BF16)
        bg_rest = sb("bg_rest", [3, 2, P])
        bg_mix = sb("bg_mix", [3, P])
        bg_rows = sb("bg_rows", [3, P], BF16)
        cls_sb = sb("cls_sb", [E_T, P])
        cls_t = sb("cls_t", [P, E_T])
        route_bias_sb = sb("route_bias_sb", [P, E_T])

        x_all = sb("x_all", [P, B, NT, P])
        h_all = sb("h_all", [P, B, NT, P])
        xn_all = sb("xn_all", [P, B, 512])
        stats1 = sb("stats1", [P, 2, NT, 6])
        stats2 = sb("stats2", [P, 2, NT, 6])
        stats = sb("stats", [P, NT, 6])
        mv = sb("mv", [P, 2, 2, NT, 2])
        ve = sb("ve", [P, 2, 2, NT])
        nm = sb("nm", [P, 2, 2, NT])
        rs = sb("rs", [P, 2, 2, NT])
        mr = sb("mr", [P, 2, 2, NT])

        COLS = GROUPS * SEGS
        delta = sb("delta", [P, GROUPS * T])
        drive = sb("drive", [P, GROUPS * T])
        H = sb("H", [P, GROUPS * T])
        h_in = sb("h_in", [P, COLS])
        h_in0 = sb("h_in0", [P, COLS])
        ends = sb("ends", [P, COLS])
        differ = sb("differ", [P, COLS])
        differ_p = sb("differ_p", [P, 1])
        ones_col = sb("ones_col", [P, 1])
        again = sb("again", [1, 1], I32)

        gu_raw = sb("gu_raw", [P, 2, PAIRS, P])
        dn_raw = sb("dn_raw", [P, E_R, INNER])
        w_hi = sb("w_hi", [P, 3, PAIRS, P], F32R)
        w_lo = sb("w_lo", [P, 3, PAIRS, P], F32R)

        z = x_all[:, 1, :, :]
        h2t = (x_all[:, 2, :, :].rearrange("p j d -> p (j d)"),
               x_all[:, 3, :, :].rearrange("p j d -> p (j d)"))
        raw_g = gu_raw[:, 0, :, :].rearrange("p k d -> p (k d)")
        raw_u = gu_raw[:, 1, :, :].rearrange("p k d -> p (k d)")
        raw_d = dn_raw[:, :, :].rearrange("p e i -> p (e i)")
        act4 = raw_g.rearrange("p (k n) -> p k n", k=4)
        silu_g = raw_u[:, 0:1024].rearrange("p (k n) -> p k n", k=2)
        f_t = raw_u[:, 1024:1536]
        zero_part = raw_d[:, 0:1024].rearrange("p (k n) -> p k n", k=2)
        out_sb = raw_d[:, 1024:1536].rearrange("p (j d) -> p j d", j=NT)
        v_t = raw_d[:, 1536:2048].rearrange("p (j d) -> p j d", j=NT)
        now_mod = sb("now_mod", [P, 2])
        now_gb = sb("now_gb", [P, 2])
        mv3 = sb("mv3", [P, NT, 2])
        ve3 = sb("ve3", [P, NT])
        nm3 = sb("nm3", [P, NT])
        mr3 = sb("mr3", [P, NT])
        rs3 = sb("rs3", [P, NT])
        h2_hi = sb("h2_hi", [P, 2, 512], F32R)
        h2_lo = sb("h2_lo", [P, 2, 512], F32R)
        lmax = sb("lmax", [P, NT])
        ls = sb("ls", [P, NT, E_T])
        ex = sb("ex", [P, NT, E_T])
        esum = sb("esum", [P, NT])
        erec = sb("erec", [P, NT])
        score = sb("score", [P, NT, E_T])
        scaled = sb("scaled", [P, NT, E_T])
        biased = sb("biased", [P, NT, E_T + 2])
        marked = sb("marked", [P, NT, E_T + 2])
        top8 = sb("top8", [P, NT, 8])
        chosen = sb("chosen", [P, NT, E_T])
        weight = sb("weight", [P, NT, E_T])
        zero_w = sb("zero_w", [P, NT])
        rest1 = sb("rest1", [P, NT, E_R + 1])
        w3 = sb("w3", [P, NT, 3, E_R + 1], BF16)
        w3t = sb("w3t", [W_ROWS, 512], BF16)
        act_hi = sb("act_hi", [P, 4, 512], F32R)
        gated = sb("gated", [P, 2, 512])
        act_lo = sb("act_lo", [P, 4, 512], F32R)

        zero_made = sem("zero_made")
        in_cond = sem("in_cond")
        in_wmod = sem("in_wmod")
        in_small = sem("in_small")
        in_x0 = sem("in_x0")
        in_x = sem("in_x")
        in_affine = sem("in_affine")
        in_w = sem("in_w")
        in_late = sem("in_late")
        in_gu = sem("in_gu")
        in_dn = sem("in_dn")
        pool_const = sem("pool_const")
        c_silu_done = sem("c_silu_done")
        ct_mm = sem("ct_mm")
        ct_done = sem("ct_done")
        mod_mm = sem("mod_mm")
        w_pad_done = sem("w_pad_done")
        ga_done = sem("ga_done")
        ga_rep_mm = sem("ga_rep_mm")
        bg_done = sem("bg_done")
        small_done = sem("small_done")
        rows_mm = sem("rows_mm")
        rows_dve = sem("rows_dve")
        rows_act = sem("rows_act")
        dve_chain = sem("dve_chain")
        moments1 = sem("moments1")
        shape1 = sem("shape1")
        pow1_done = sem("pow1_done")
        rstd1_done = sem("rstd1_done")
        z1_done = sem("z1_done")
        spread1 = sem("spread1")
        spread2 = sem("spread2")
        h_chain = sem("h_chain")
        h_done = sem("h_done")
        moments2 = sem("moments2")
        shape2 = sem("shape2")
        pow2_done = sem("pow2_done")
        rstd2_done = sem("rstd2_done")
        z2_done = sem("z2_done")
        z2t_done = sem("z2t_done")
        xnt_done = sem("xnt_done")
        proj_done = sem("proj_done")
        delta_out = sem("delta_out")
        drive_out = sem("drive_out")
        step_mm = sem("step_mm")
        step_h = sem("step_h")
        step_in = sem("step_in")
        verdict_mm = sem("verdict_mm")
        verdict = sem("verdict")
        more_mm = sem("more_mm")
        more_h = sem("more_h")
        more_in = sem("more_in")
        more_y = sem("more_y")
        more_v = sem("more_v")
        side_mm = sem("side_mm")
        side_hi = sem("side_hi")
        side_lo = sem("side_lo")
        side_gate = sem("side_gate")
        res_chain = sem("res_chain")
        res_done = sem("res_done")

        gate_mm = sem("gate_mm")
        up_mm = sem("up_mm")
        down_mm = sem("down_mm")
        route_mm = sem("route_mm")
        zero_mm = sem("zero_mm")
        silu_done = sem("silu_done")
        gated_done = sem("gated_done")
        act_done = sem("act_done")
        hi_done = sem("hi_done")
        lo_done = sem("lo_done")
        y_mm = sem("y_mm")
        zt_mm = sem("zt_mm")
        logit_mm = sem("logit_mm")
        weight_mm = sem("weight_mm")
        ft_mm = sem("ft_mm")
        pre_chain = sem("pre_chain")
        var3_done = sem("var3_done")
        rstd3_done = sem("rstd3_done")
        z_done = sem("z_done")
        v_done = sem("v_done")
        x1_done = sem("x1_done")
        stats3_done = sem("stats3_done")
        nm3_done = sem("nm3_done")
        pow3_done = sem("pow3_done")
        zero_done = sem("zero_done")
        h2t_done = sem("h2t_done")
        h2_hi_done = sem("h2_hi_done")
        h2_lo_done = sem("h2_lo_done")
        shifted_done = sem("shifted_done")
        exp_done = sem("exp_done")
        weight_done = sem("weight_done")
        weight_t_done = sem("weight_t_done")
        f_done = sem("f_done")
        gb_ready = sem("gb_ready")
        out_ready = sem("out_ready")
        out_dma = sem("out_dma")

        out_tiles = out.rearrange("b (j p) d -> b p j d", p=P)
        gu_view = gate_up[0:E_R].rearrange("(pair e2) (gu i) h -> e2 gu i pair h", e2=2, gu=2)
        N_SETUP_CONST, N_POOL_CONST = 11, 22
        LOW, GONE = -3.0e38, 3.0e38

        def wait(eng, s, value):
            if isinstance(value, int) and value <= 0:
                return
            eng.wait_ge(s, value)

        def wait_apart(eng, s, value):
            if not isinstance(value, int):
                eng.wait_ge(in_x, 16 * 3)
            eng.wait_ge(s, value)

        def row(k, b):
            return rows[:, k, b, :].unsqueeze(1).broadcast_to([P, NT, P])

        N_WEIGHTS, N_GATES = 3 * PAIRS // 4, 2 * B
        SIDE_WORK = [("weights", n) for n in range(N_WEIGHTS)] + [("gate", n) for n in range(N_GATES)]
        NS = len(SIDE)

        def side_read(n):
            kind, m = SIDE_WORK[n]
            return (side_lo, m + 1) if kind == "weights" else (side_gate, m + 1)

        ROW_ORDER = [(R_CA1, CA1, 0), (R_SA, SA, 0), (R_CA1, CA1, 1), (R_SA, SA, 1), (R_GA, GA, 0), (R_GA, GA, 1)]
        SWEEP_STEPS = 2 * SEG_LEN

        def rows_to(k):
            b0 = 4 * ROW_ORDER[k][2]
            return rows[:, ROW_ORDER[k][0], b0:b0 + 4, :].rearrange("p b d -> p (b d)")

        block = ctx.enter_context(nc.Block())

        @block.sync
        def _(sp):
            sp.dma_start(wmod_sb[:, :], wmod).then_inc(in_wmod, 16)
            for k in range(4):
                sp.dma_start(x_all[:, 2 * k:2 * k + 2, :, :].rearrange("p b j d -> p (b j) d"),
                             x[2 * k:2 * k + 2].rearrange("b (j p) d -> p (b j) d", p=P)).then_inc(in_x if k else in_x0, 16)
            sp.dma_start(gb_col[:, 0:1], ln_gamma.unsqueeze(1)).then_inc(in_affine, 16)
            sp.dma_start(gb_col[:, 1:2], ln_beta.unsqueeze(1)).then_inc(in_affine, 16)
            sp.wait_ge(w_pad_done, 1)
            sp.dma_start(w_pad[:, W_PAD:W_PAD + S], w_delta).then_inc(in_w, 16)
            sp.dma_start(w_pad[:, W_PAD + S:W_PAD + 2 * S], w_in).then_inc(in_w, 16)
            sp.dma_start(small[:, 0:S], A).then_inc(in_small, 16)
            sp.dma_start(small[:, S:S + P], C).then_inc(in_small, 16)
            sp.dma_start(small[:, S + P:S + P + 1], b_delta.unsqueeze(1)).then_inc(in_small, 16)
            sp.dma_start(small[:, S + P + 1:S + P + 2], b_in.unsqueeze(1)).then_inc(in_small, 16)
            sp.dma_start(wg_sb[:, :], w_gate).then_inc(in_late, 16)
            sp.dma_start(bg3[:, :], b_gate.unsqueeze(0).broadcast_to([3, P])).then_inc(in_late, 16)
            sp.dma_start(cls_sb[:, :], classifier).then_inc(in_late, 16)
            sp.dma_start(route_bias_sb[:, :], route_bias.unsqueeze(0).broadcast_to([P, E_T])).then_inc(in_late, 16)
            for e2 in range(2):
                for gu in range(2):
                    sp.dma_start(gu_raw[e2 * INNER:(e2 + 1) * INNER, gu, :, :], gu_view[e2, gu]).then_inc(in_gu, 16)
            sp.dma_start(dn_raw[:, :, :], down.rearrange("e h i -> h e i")).then_inc(in_dn, 16)

            with sp.Fori(0, B) as b:
                sp.wait_ge(out_ready, b + 1)
                sp.dma_start(out_tiles[bass.ds(b, 1)].rearrange("a p j d -> p (a j) d"), out_sb[:, :, :]).then_inc(out_dma, 16)
            sp.wait_ge(out_dma, 16 * B)

        @block.gpsimd
        def _(pool):
            g = nc.gpsimd
            made = [0]

            def const(ins):
                ins.then_inc(pool_const, 1)
                made[0] += 1
                pool.wait_ge(pool_const, made[0])

            const(g.memset(minus_half[:, :], -0.5))
            const(g.memset(ident[:, :], 0.0))
            const(g.affine_select(out=ident[:, :], in_=ident[:, :], compare_op=ALU.not_equal, fill=1.0, base=0,
                                  pattern=[[-1, P + S]], channel_multiplier=1))
            const(g.memset(minus_one[:, :], -1.0))
            const(g.memset(eps[:, :], EPS))
            const(g.memset(spread_rows[:, :, :, :, :], 0.0))
            for which in range(2):
                const(g.tensor_copy(spread_rows[:, which, :, which, :], ident[0:S, 0:S].unsqueeze(1).broadcast_to([S, BG, S])))
            const(g.memset(own_batch[:, :], 1.0))
            const(g.affine_select(out=own_batch[:, :], in_=own_batch[:, :], compare_op=ALU.is_ge, fill=0.0, base=0,
                                  pattern=[[-2 * S, BG]], channel_multiplier=1))
            const(g.affine_select(out=own_batch[:, :], in_=own_batch[:, :], compare_op=ALU.is_ge, fill=0.0, base=2 * S - 1,
                                  pattern=[[2 * S, BG]], channel_multiplier=-1))
            assert made[0] == N_SETUP_CONST
            const(g.memset(ones3[:, :], 1.0))
            const(g.memset(h_in0[:, :], 0.0))
            const(g.tensor_copy(ident_bf[:, :], ident[:, 0:P]))

            def select_pairs(part):
                at = pick_pair[:, :, :].rearrange("r pair (e2 i) -> r pair e2 i", e2=2)
                const(g.affine_select(out=at, in_=at, compare_op=ALU.not_equal, fill=1.0, base=-(E_R + 1) * part,
                                      pattern=[[-2, PAIRS], [-1, 2], [0, INNER]], channel_multiplier=1))

            def rstd(norm, par, b, before, shape, powed, done, used):
                pool.wait_ge(before, b + 1)
                wait(pool, used, b - 1)
                g.tensor_tensor(ve[:, norm, par, :], mv[:, norm, par, :, 1], eps[:, :], ALU.add)
                g.tensor_tensor(nm[:, norm, par, :], mv[:, norm, par, :, 0], minus_one[:, :], ALU.mult).then_inc(shape, 1)
                pool.wait_ge(shape, b + 1)
                g.tensor_tensor(rs[:, norm, par, :], ve[:, norm, par, :], minus_half[:, :], ALU.pow).then_inc(powed, 1)
                pool.wait_ge(powed, b + 1)
                g.tensor_tensor(mr[:, norm, par, :], nm[:, norm, par, :], rs[:, norm, par, :], ALU.mult).then_inc(done, 1)

            def first(b, par):
                rstd(0, par, b, moments1, shape1, pow1_done, rstd1_done, z1_done)

            def second(b, par):
                rstd(1, par, b, moments2, shape2, pow2_done, rstd2_done, z2_done)

            first(0, 0)
            first(1, 1)
            first(2, 0)
            second(0, 0)
            first(3, 1)
            second(1, 1)
            first(4, 0)
            with pool.Fori(1, (B - 4) // 2) as i:
                second(i * 2, 0)
                first(i * 2 + 3, 1)
                second(i * 2 + 1, 1)
                first(i * 2 + 4, 0)
            second(B - 4, 0)
            first(B - 1, 1)
            for b in range(B - 3, B):
                second(b, b % 2)
            pool.wait_ge(rstd2_done, B)
            const(g.memset(pick_pair[:, :, :], 0.0))
            for part in range(3):
                select_pairs(part)
            const(g.memset(pick_zero[:, :], 0.0))
            for part in range(3):
                const(g.affine_select(out=pick_zero[:, :], in_=pick_zero[:, :], compare_op=ALU.not_equal, fill=1.0,
                                      base=-(E_R + 1) * part - E_R, pattern=[[0, P]], channel_multiplier=1))
            assert made[0] == N_POOL_CONST, made[0]
            with pool.Fori(0, B) as b:
                pool.wait_ge(z2_done, b + 1)
                g.tensor_tensor(h_all[:, b, :, :], h_all[:, b, :, :], row(R_GA, b), ALU.mult).then_inc(res_chain, 1)
                pool.wait_ge(res_chain, b + 1)
                g.tensor_tensor(h_all[:, b, :, :], h_all[:, b, :, :], x_all[:, b, :, :], ALU.add).then_inc(res_done, 1)

            def prepare_x1(n):
                pool.wait_ge(v_done, n + 1)
                g.tensor_tensor(h_all[:, n, :, :], v_t[:, :, :], h_all[:, n, :, :], ALU.add).then_inc(x1_done, 1)

            def prepare_rstd(n):
                pool.wait_ge(stats3_done, n + 1)
                wait(pool, z_done, n)
                g.tensor_tensor(ve3[:, :], mv3[:, :, 1], eps[:, :], ALU.add)
                g.tensor_tensor(nm3[:, :], mv3[:, :, 0], minus_one[:, :], ALU.mult).then_inc(nm3_done, 1)
                pool.wait_ge(nm3_done, n + 1)
                g.tensor_tensor(rs3[:, :], ve3[:, :], minus_half[:, :], ALU.pow).then_inc(pow3_done, 1)
                pool.wait_ge(pow3_done, n + 1)
                g.tensor_tensor(mr3[:, :], nm3[:, :], rs3[:, :], ALU.mult).then_inc(rstd3_done, 1)

            def prepare_lo(n, par):
                pool.wait_ge(h2_hi_done, n + 1)
                g.tensor_tensor(h2_lo[:, par, :], h2t[par][:, :], h2_hi[:, par, :].bitcast(F32), ALU.subtract).then_inc(h2_lo_done, 1)

            def experts(c, par, has_next, has_two):
                for p in range(PAIRS):
                    q = c * PAIRS + p
                    if has_next or p < PAIRS - 1:
                        wait(pool, down_mm, q - 3)
                        pool.wait_ge(hi_done, q + 1)
                        g.tensor_tensor(act_lo[:, p % 4, :], act4[:, p % 4, :], act_hi[:, p % 4, :].bitcast(F32),
                                        ALU.subtract).then_inc(lo_done, 1)
                    if has_next and p == 0:
                        prepare_rstd(c + 1)
                    if has_next and p == 5:
                        prepare_lo(c + 1, 1 - par)
                    if has_two and p == 3:
                        prepare_x1(c + 2)

            pool.wait_ge(res_done, B)
            prepare_rstd(0)
            prepare_x1(1)
            prepare_lo(0, 0)
            experts(0, 0, True, True)
            with pool.Fori(0, (B - 4) // 2) as i:
                experts(i * 2 + 1, 1, True, True)
                experts(i * 2 + 2, 0, True, True)
            experts(B - 3, 1, True, True)
            experts(B - 2, 0, True, False)
            experts(B - 1, 1, False, False)

        @block.scalar
        def _(act):
            a = nc.scalar
            act.dma_start(c_row[:, :], cond).then_inc(in_cond, 16)
            act.wait_ge(pool_const, 1)
            a.activation(warm[:, 0:1], minus_half[:, 0:1], ACT.Silu)
            act.wait_ge(in_cond, 16)
            a.activation(c_silu[:, :], c_row[:, :], ACT.Silu).then_inc(c_silu_done, 1)
            a.activation(warm[:, 1:2], minus_half[:, 0:1], ACT.Sigmoid)

            def take_rows(k):
                act.wait_ge(rows_mm, k + 1)
                add = {"bias": ones_col[:, 0:1]} if ROW_ORDER[k][1] == CA1 else {}
                a.activation(rows_to(k), bank[:, ROWS_B[k], :], ACT.Identity, **add).then_inc(rows_act, 1)

            def first(b, par):
                wait_apart(act, rstd1_done, b + 1)
                for j in range(NT):
                    done = a.activation(h_all[:, b, j, :], x_all[:, b, j, :], ACT.Identity,
                                        bias=mr[:, 0, par, j:j + 1], scale=rs[:, 0, par, j:j + 1])
                done.then_inc(z1_done, 1)

            def second(b, par):
                wait_apart(act, rstd2_done, b + 1)
                for j in range(NT):
                    done = a.activation(xn_all[:, b, j * P:(j + 1) * P], h_all[:, b, j, :], ACT.Identity,
                                        bias=mr[:, 1, par, j:j + 1], scale=rs[:, 1, par, j:j + 1])
                done.then_inc(z2_done, 1)

            def affine(b, par):
                wait_apart(act, z2t_done, b + 1)
                a.activation(xn_all[:, b, :], bank[:, MISC[par], :], ACT.Identity,
                             bias=gb_col[:, 1:2], scale=gb_col[:, 0:1]).then_inc(xnt_done, 1)

            first(0, 0)
            first(1, 1)
            act.wait_ge(w_pad_done, 1)
            take_rows(2)
            take_rows(3)
            first(2, 0)
            take_rows(4)
            take_rows(5)
            second(0, 0)
            act.wait_ge(in_affine, 32)
            first(3, 1)
            second(1, 1)
            affine(0, 0)
            with act.Fori(0, (B - 4) // 2) as i:
                first(i * 2 + 4, 0)
                second(i * 2 + 2, 0)
                affine(i * 2 + 1, 1)
                first(i * 2 + 5, 1)
                second(i * 2 + 3, 1)
                affine(i * 2 + 2, 0)
            second(B - 2, 0)
            affine(B - 3, 1)
            affine(B - 2, 0)
            affine(B - 1, 1)
            act.wait_ge(small_done, 1)
            for g in range(GROUPS):
                act.wait_ge(proj_done, g + 1)
                a.activation(delta[:, g * T:(g + 1) * T], bank[:, PROJ_B[g], :], ACT.Sigmoid,
                             bias=small_rep[:, S + P:S + P + 1]).then_inc(delta_out, 1)

            for n in range(SWEEP_STEPS):
                k = n % SEG_LEN
                act.wait_ge(step_mm, n + 1)
                a.activation(H[:, k::SEG_LEN], bank[:, SCAN[n % 2], 0:COLS], ACT.Tanh).then_inc(step_h, 1)
                if 0 <= n - 1 < len(SIDE_WORK):
                    kind, m = SIDE_WORK[n - 1]
                    act.wait_ge(side_mm, n)
                    src = bank[:, SIDE[(n - 1) % NS], :]
                    if kind == "weights":
                        a.activation(w_hi[:, m // 4, 4 * (m % 4):4 * (m % 4) + 4, :].rearrange("p k d -> p (k d)"),
                                     src, ACT.Identity).then_inc(side_hi, 1)
                    else:
                        half = 256 * (m % 2)
                        a.activation(xn_all[:, m // 2, half:half + 256], src[:, 0:256], ACT.Sigmoid).then_inc(side_gate, 1)
            a.activation(warm[:, 2:3], minus_half[:, 0:1], ACT.Exp)
            act.wait_ge(verdict, 1)
            go_on = act.value_load(again[0:1, 0:1])
            with act.If(go_on != 0):
                with act.Fori(0, SEGS - 2) as s:
                    with act.Fori(0, SEG_LEN) as k:
                        act.wait_ge(more_mm, s * SEG_LEN + k + 1)
                        a.activation(H[:, bass.ds(k, COLS, SEG_LEN)], bank[:, SCAN[0], 0:COLS], ACT.Tanh).then_inc(more_h, 1)

            def prepare_z(n):
                wait_apart(act, rstd3_done, n + 1)
                wait(act, zt_mm, n)
                for j in range(NT):
                    done = a.activation(z[:, j, :], h_all[:, n, j, :], ACT.Identity,
                                        bias=mr3[:, j:j + 1], scale=rs3[:, j:j + 1])
                done.then_inc(z_done, 1)

            def prepare_h2(n, par):
                act.wait_ge(zt_mm, n + 1)
                wait(act, zero_done, n - 1)
                a.activation(h2t[par][:, :], bank[:, PREP_B, :], ACT.Identity,
                             bias=now_mod[:, 0:1], scale=now_mod[:, 1:2]).then_inc(h2t_done, 1)
                act.wait_ge(h2t_done, n + 1)
                a.activation(h2_hi[:, par, :], h2t[par][:, :], ACT.Identity).then_inc(h2_hi_done, 1)

            def prepare_exp(n):
                act.wait_ge(shifted_done, n + 1)
                a.activation(ex[:, :, :], ls[:, :, :], ACT.Exp).then_inc(exp_done, 1)

            def prepare_weights(n):
                act.wait_ge(weight_mm, n + 1)
                wait(act, route_mm, n * PAIRS)
                wait(act, zero_mm, n)
                a.activation(w3t[:, :], bank[0:W_ROWS, PREP_B, :].bitcast(BF16)[:, 0:512], ACT.Identity).then_inc(weight_t_done, 1)

            def high_part(q, slot):
                wait(act, down_mm, q - 3)
                act.wait_ge(act_done, q + 1)
                a.activation(act_hi[:, slot, :], act4[:, slot, :], ACT.Identity).then_inc(hi_done, 1)

            def experts(c, par, has_prev, has_next):
                for p in range(PAIRS):
                    q = c * PAIRS + p
                    if has_prev and p == 0:
                        prepare_weights(c)
                    wait(act, gated_done, q - 1)
                    act.wait_ge(gate_mm, q + 1)
                    a.activation(silu_g[:, p % 2, :], bank[:, GATE_B[p % 2], :], ACT.Silu).then_inc(silu_done, 1)
                    if not has_prev and p == 1:
                        prepare_weights(0)
                    if has_next and p == 9:
                        prepare_exp(c + 1)
                    if p > 0 or has_prev:
                        high_part(q - 1, (p - 1) % 4)
                    if has_next and p == 3:
                        prepare_z(c + 1)
                    if has_next and p == 5:
                        prepare_h2(c + 1, 1 - par)

            prepare_h2(0, 0)
            prepare_exp(0)
            experts(0, 0, False, True)
            with act.Fori(0, (B - 2) // 2) as i:
                experts(i * 2 + 1, 1, True, True)
                experts(i * 2 + 2, 0, True, True)
            experts(B - 1, 1, True, False)
            high_part(B * PAIRS - 1, (PAIRS - 1) % 4)

        @block.vector
        def _(dve):
            v = nc.vector
            chained = [0]

            def chain(ins):
                chained[0] += 1
                ins.then_inc(dve_chain, 1)
                dve.wait_ge(dve_chain, chained[0])

            v.memset(zero_bf[:, :], 0.0).then_inc(zero_made, 1)
            v.memset(ones_col[:, :], 1.0)
            v.memset(a_block[:, :, :, :], 0.0)
            v.memset(biased[:, :, :], LOW)
            v.memset(w_pad[:, :], 0.0).then_inc(w_pad_done, 1)

            def spread(source, to, done):
                for j in range(NT):
                    last = v.bn_stats(to[:, j, :], source(j))
                last.then_inc(done, 1)

            def moments(norm, par, source, done):
                for j in range(NT):
                    last = v.bn_aggr(mv[:, norm, par, j, :], source[:, par, j, :])
                last.then_inc(done, 1)

            dve.wait_ge(ct_mm, 1)
            v.tensor_copy(c_silu_t[:, :], bank[:, SETUP_B, 0:B]).then_inc(ct_done, 1)
            dve.wait_ge(in_x0, 16)
            spread(lambda j: x_all[:, 0, j, :], stats1[:, 0], spread1)
            dve.wait_ge(spread1, 1)
            moments(0, 0, stats1, moments1)
            spread(lambda j: x_all[:, 1, j, :], stats1[:, 1], spread1)
            dve.wait_ge(spread1, 2)
            moments(0, 1, stats1, moments1)

            def take_rows(k):
                dve.wait_ge(rows_mm, k + 1)
                v.tensor_scalar_add(rows_to(k), bank[:, ROWS_B[k], :], 1.0 if ROW_ORDER[k][1] == CA1 else 0.0).then_inc(rows_dve, 1)

            take_rows(0)
            take_rows(1)
            dve.wait_ge(mod_mm, 1)
            raw = bank[:, SETUP_B, GA * B:NMOD * B].rearrange("p (m b) -> p m b", b=B)
            chain(v.tensor_copy(modt[:, GA:NMOD, :], raw))
            chain(v.tensor_scalar_add(modt[:, CB1, :], modt[:, CB1, :], 1.0))
            both = modt[:, GA:GB + 1:GB - GA, :]
            chain(v.tensor_scalar(mod_tmp[:, 0, :, :], both, 0.0, 2.0, ALU.is_ge, ALU.mult))
            chain(v.tensor_scalar_add(mod_tmp[:, 0, :, :], mod_tmp[:, 0, :, :], -1.0))
            chain(v.tensor_tensor(mod_tmp[:, 1, :, :], both, mod_tmp[:, 0, :, :], ALU.mult))
            chain(v.scalar_tensor_tensor(out=both, in0=mod_tmp[:, 1, :, :], scalar=MOD_FLOOR,
                                         in1=mod_tmp[:, 0, :, :], op0=ALU.max, op1=ALU.mult))
            v.tensor_copy(ga_rep[:, :, :, :], modt[:, GA, :].rearrange("p (b4 g) -> p g b4", g=GROUPS).unsqueeze(3)
                          .broadcast_to([P, GROUPS, BG, 2 * S])).then_inc(ga_done, 1)

            def scale(b, par, has_last):
                if has_last:
                    dve.wait_ge(spread2, b)
                dve.wait_ge(z1_done, b + 1)
                v.tensor_tensor(h_all[:, b, :, :], h_all[:, b, :, :], row(R_CA1, b), ALU.mult).then_inc(h_chain, 1)
                if has_last:
                    moments(1, 1 - par, stats2, moments2)

            def shift(b, par, has_ahead):
                if has_ahead:
                    dve.wait_ge(spread1, b + 3)
                dve.wait_ge(h_chain, b + 1)
                v.tensor_tensor(h_all[:, b, :, :], h_all[:, b, :, :], row(R_SA, b), ALU.add).then_inc(h_done, 1)
                if has_ahead:
                    moments(0, par, stats1, moments1)

            def spread_h(b, par):
                dve.wait_ge(in_x, 16 * 3)
                dve.wait_ge(h_done, b + 1)
                spread(lambda j: h_all[:, b, j, :], stats2[:, par], spread2)

            def step(b, par, has_last, has_ahead):
                scale(b, par, has_last)
                if has_ahead:
                    spread(lambda j: x_all[:, b + 2, j, :], stats1[:, par], spread1)
                shift(b, par, has_ahead)
                spread_h(b, par)

            dve.wait_ge(in_x, 16 * 3)
            dve.wait_ge(rows_dve, 2)
            step(0, 0, False, True)
            step(1, 1, True, True)
            dve.wait_ge(rows_act, 2)
            with dve.Fori(0, (B - 4) // 2) as i:
                step(i * 2 + 2, 0, True, True)
                step(i * 2 + 3, 1, True, True)
            step(B - 2, 0, True, False)
            step(B - 1, 1, True, False)
            dve.wait_ge(spread2, B)
            dve.wait_ge(rstd2_done, B - 2)
            moments(1, 1, stats2, moments2)

            dve.wait_ge(ga_rep_mm, 1)
            v.tensor_copy(small_rep[:, :], bank[:, SETUP_B, AT_SMALL:AT_SMALL + S + P + 1]).then_inc(small_done, 1)
            chain(v.tensor_copy(cls_t[:, :], bank[:, SETUP_B, AT_CLS:AT_CLS + E_T]))
            v.tensor_tensor(a_block[:, :, 0, :], small_rep[:, 0:S].unsqueeze(1).broadcast_to([P, BG, S]),
                            own_batch[:, :].unsqueeze(2).broadcast_to([P, BG, S]), ALU.mult)
            chain(v.tensor_tensor(c_ga[:, :, :], bank[:, SETUP_B, AT_GA:AT_GA + GROUPS * P].rearrange("p (g d) -> p g d", g=GROUPS),
                                  small_rep[:, S:S + P].unsqueeze(1).broadcast_to([P, GROUPS, P]), ALU.mult))
            dve.wait_ge(rstd2_done, B)
            dve.wait_ge(z2_done, B - 1)
            for j in range(NT):
                done = v.tensor_scalar(xn_all[:, B - 1, j * P:(j + 1) * P], h_all[:, B - 1, j, :],
                                       rs[:, 1, 1, j:j + 1], mr[:, 1, 1, j:j + 1], ALU.mult, ALU.add)
            done.then_inc(z2_done, 1)
            dve.wait_ge(in_late, 64)
            chain(v.tensor_copy(bg_part[:, 0, :], bg3[:, :]))
            chain(v.tensor_tensor(bg_rest[:, 0, :], bg3[:, :], bg_part[:, 0, :], ALU.subtract))
            chain(v.tensor_copy(bg_part[:, 1, :], bg_rest[:, 0, :]))
            chain(v.tensor_tensor(bg_rest[:, 1, :], bg_rest[:, 0, :], bg_part[:, 1, :], ALU.subtract))
            chain(v.tensor_copy(bg_part[:, 2, :], bg_rest[:, 1, :]))
            chain(v.tensor_scalar_mul(bg_mix[:, :], bg_part[:, 0, :], ident[0:3, 0:1]))
            chain(v.scalar_tensor_tensor(out=bg_mix[:, :], in0=bg_part[:, 1, :], scalar=ident[0:3, 1:2], in1=bg_mix[:, :],
                                         op0=ALU.mult, op1=ALU.add))
            v.scalar_tensor_tensor(out=bg_rows[:, :], in0=bg_part[:, 2, :], scalar=ident[0:3, 2:3], in1=bg_mix[:, :],
                                   op0=ALU.mult, op1=ALU.add).then_inc(bg_done, 1)
            for g in range(GROUPS):
                dve.wait_ge(delta_out, g + 1)
                v.tensor_scalar(drive[:, g * T:(g + 1) * T], bank[:, PROJ_B[g], :], small_rep[:, S + P:S + P + 1],
                                None, ALU.add).then_inc(drive_out, 1)

            H3 = H[:, :].rearrange("p (g t) -> p g t", g=GROUPS)
            delta3 = delta[:, :].rearrange("p (g t) -> p g t", g=GROUPS)

            def make_v(n):
                return v.tensor_tensor(v_t[:, :, :].rearrange("p j d -> p (j d)"), bank[:, PREP_B, :], xn_all[:, n, :], ALU.mult)

            def first_in(to):
                return v.tensor_tensor(to[:, :].rearrange("p (g c) -> p g c", g=GROUPS)[:, :, 1:SEGS],
                                       H3[:, :, SEG_LEN - 1:T - SEG_LEN:SEG_LEN], delta3[:, :, SEG_LEN::SEG_LEN], ALU.mult)

            dve.wait_ge(delta_out, GROUPS)
            for n in range(SWEEP_STEPS):
                k = n % SEG_LEN
                dve.wait_ge(step_h, n + 1)
                if k < SEG_LEN - 1:
                    v.tensor_tensor(h_in[:, :], H[:, k::SEG_LEN], delta[:, k + 1::SEG_LEN], ALU.mult).then_inc(step_in, 1)
                elif n < SWEEP_STEPS - 1:
                    first_in(h_in0).then_inc(step_in, 1)
                    v.tensor_copy(ends[:, :], H[:, k::SEG_LEN])
                else:
                    chain(v.tensor_tensor(differ[:, :], H[:, k::SEG_LEN], ends[:, :], ALU.not_equal))
                    v.tensor_reduce(differ_p[:, :], differ[:, :], AX, ALU.max).then_inc(step_in, 1)
                if n == N_WEIGHTS + 2:
                    v.tensor_tensor(c_batch[:, :, :].rearrange("p (b4 g) d -> p b4 g d", g=GROUPS),
                                    c_ga[:, :, :].unsqueeze(1).broadcast_to([P, BG, GROUPS, P]),
                                    own_batch[:, :].unsqueeze(2).unsqueeze(3).broadcast_to([P, BG, GROUPS, P]),
                                    ALU.mult)
                if 0 <= n - 2 < N_WEIGHTS:
                    m = SIDE_WORK[n - 2][1]
                    dve.wait_ge(side_hi, m + 1)
                    part = (slice(None), m // 4, slice(4 * (m % 4), 4 * (m % 4) + 4), slice(None))
                    v.tensor_tensor(w_lo[part].rearrange("p k d -> p (k d)"), bank[:, SIDE[(n - 2) % NS], :],
                                    w_hi[part].rearrange("p k d -> p (k d)").bitcast(F32), ALU.subtract).then_inc(side_lo, 1)
            dve.wait_ge(verdict_mm, 1)
            v.tensor_copy(again[:, :], bank[0:1, SCAN[0], 0:1]).then_inc(verdict, 1)
            dve.wait_ge(side_gate, N_GATES)
            dve.wait_ge(y_mm, 1)
            make_v(0).then_inc(v_done, 1)
            dve.wait_ge(verdict, 1)
            go_on = dve.value_load(again[0:1, 0:1])
            with dve.If(go_on != 0):
                with dve.Fori(0, SEGS - 2) as s:
                    first_in(h_in)
                    v.memset(h_in[:, 0:COLS:SEGS], 0.0).then_inc(more_in, 1)
                    with dve.Fori(0, SEG_LEN - 1) as k:
                        dve.wait_ge(more_h, s * SEG_LEN + k + 1)
                        v.tensor_tensor(h_in[:, :], H[:, bass.ds(k, COLS, SEG_LEN)], delta[:, bass.ds(k + 1, COLS, SEG_LEN)],
                                        ALU.mult).then_inc(more_in, 1)
                    dve.wait_ge(more_h, s * SEG_LEN + SEG_LEN)
                dve.wait_ge(more_y, 1)
                dve.wait_ge(v_done, 1)
                make_v(0).then_inc(more_v, 1)
                dve.wait_ge(more_v, 1)

            PRE = 15
            at = [0]

            def mark(ins):
                at[0] += 1
                ins.then_inc(pre_chain, 1)

            def after(n):
                dve.wait_ge(pre_chain, n * PRE + at[0])

            def prepare_v(n):
                dve.wait_ge(y_mm, n + 1)
                wait(dve, x1_done, n)
                make_v(n).then_inc(v_done, 1)

            def prepare_stats(n):
                dve.wait_ge(in_x, 16 * 3)
                dve.wait_ge(x1_done, n + 1)
                for j in range(NT):
                    last = v.bn_stats(stats[:, j, :], h_all[:, n, j, :])
                last.then_inc(var3_done, 1)

            def prepare_moments(n):
                dve.wait_ge(in_x, 16 * 3)
                dve.wait_ge(var3_done, n + 1)
                wait(dve, rstd3_done, n)
                for j in range(NT):
                    last = v.bn_aggr(mv3[:, j, :], stats[:, j, :])
                    if j == 0:
                        v.tensor_copy(now_mod[:, :], modt[:, SB_:CB1 + 1, n])
                last.then_inc(stats3_done, 1)

            def over(t):
                return t.unsqueeze(2).broadcast_to([P, NT, E_T])

            def prepare_shift(n):
                dve.wait_ge(logit_mm, n + 1)
                logits = bank[:, PREP_B, 0:NT * E_T].rearrange("p (j e) -> p j e", j=NT)
                mark(v.tensor_reduce(lmax[:, :], logits, AX, ALU.max))
                after(n)
                v.tensor_tensor(ls[:, :, :], logits, over(lmax[:, :]), ALU.subtract).then_inc(shifted_done, 1)

            def prepare_sum(n):
                dve.wait_ge(exp_done, n + 1)
                mark(v.tensor_reduce(esum[:, :], ex[:, :, :], AX, ALU.add))
                after(n)
                mark(v.reciprocal(erec[:, :], esum[:, :]))

            def prepare_scores(n):
                after(n)
                mark(v.tensor_tensor(score[:, :, :], ex[:, :, :], over(erec[:, :]), ALU.mult))
                after(n)
                mark(v.tensor_tensor(biased[:, :, 0:E_T], score[:, :, :],
                                     route_bias_sb[:, :].unsqueeze(1).broadcast_to([P, NT, E_T]), ALU.add))

            def prepare_top(n):
                after(n)
                v.tensor_scalar_mul(scaled[:, :, 0:E_R], score[:, :, 0:E_R], ROUTE_SCALE)
                for j in range(NT):
                    last = v.max(top8[:, j, :], biased[:, j, 0:E_T])
                mark(last)

            def prepare_mark(n):
                after(n)
                mark(v.memset(top8[:, :, TOP_K:8], LOW))
                after(n)
                v.tensor_scalar_mul(scaled[:, :, E_R:E_T], score[:, :, E_R:E_T], ROUTE_SCALE)
                for j in range(NT):
                    last = v.match_replace(marked[:, j, :], top8[:, j, :], biased[:, j, :], GONE)
                mark(last)

            def prepare_chosen(n):
                after(n)
                mark(v.tensor_tensor(chosen[:, :, :], marked[:, :, 0:E_T], biased[:, :, 0:E_T], ALU.not_equal))

            def prepare_weights(n):
                after(n)
                mark(v.tensor_tensor(weight[:, :, :], chosen[:, :, :], scaled[:, :, :], ALU.mult))
                after(n)
                mark(v.tensor_reduce(zero_w[:, :], weight[:, :, E_R:E_T], AX, ALU.add))

            def prepare_part1(n):
                after(n)
                mark(v.tensor_copy(weight[:, :, E_R], zero_w[:, :]))
                after(n)
                mark(v.tensor_copy(w3[:, :, 0, :], weight[:, :, 0:E_R + 1]))

            def prepare_part2(n):
                after(n)
                mark(v.tensor_tensor(rest1[:, :, :], weight[:, :, 0:E_R + 1], w3[:, :, 0, :], ALU.subtract))
                after(n)
                mark(v.tensor_copy(w3[:, :, 1, :], rest1[:, :, :]))

            def prepare_part3(n):
                after(n)
                v.tensor_tensor(w3[:, :, 2, :], rest1[:, :, :], w3[:, :, 1, :], ALU.subtract).then_inc(weight_done, 1)
                assert at[0] == PRE, at[0]

            def zero_experts(c, par):
                wait(dve, f_done, c - 1)
                v.tensor_scalar_mul(now_gb[:, par:par + 1], modt[:, GB, bass.ds(c, 1)], 1.0).then_inc(gb_ready, 1)
                dve.wait_ge(zero_mm, c + 1)
                dve.wait_ge(gb_ready, c + 1)
                v.scalar_tensor_tensor(out=zero_part[:, par, :], in0=h2t[par][:, :], scalar=now_gb[:, par:par + 1],
                                       in1=bank[:, PREP_B, :], op0=ALU.mult, op1=ALU.mult).then_inc(zero_done, 1)

            def leave_down(c, par):
                dve.wait_ge(down_mm, (c + 1) * PAIRS)
                dve.wait_ge(zero_done, c + 1)
                wait(dve, ft_mm, c)
                v.scalar_tensor_tensor(out=f_t[:, :], in0=bank[:, DOWN_B, :], scalar=now_gb[:, par:par + 1],
                                       in1=zero_part[:, par, :], op0=ALU.mult, op1=ALU.add).then_inc(f_done, 1)

            def finish(c):
                dve.wait_ge(ft_mm, c + 1)
                wait(dve, out_dma, 16 * c)
                v.tensor_tensor(out_sb[:, :, :].rearrange("p j d -> p (j d)"), bank[:, PREP_B, :],
                                h_all[:, c, :, :].rearrange("p j d -> p (j d)"), ALU.add).then_inc(out_ready, 1)

            def experts(c, par, has_prev, has_next, has_two):
                for p in range(PAIRS):
                    q = c * PAIRS + p
                    if has_prev and p == 3:
                        leave_down(c - 1, 1 - par)
                    dve.wait_ge(silu_done, q + 1)
                    dve.wait_ge(up_mm, q + 1)
                    wait(dve, act_done, q - 1)
                    v.tensor_tensor(gated[:, p % 2, :], silu_g[:, p % 2, :], bank[:, UP_B[p % 2], :], ALU.mult).then_inc(gated_done, 1)
                    if has_prev and has_next and p == 0:
                        prepare_stats(c + 1)
                    if has_next and p == 1:
                        prepare_moments(c + 1)
                    if has_two and p == 2:
                        prepare_v(c + 2)
                    if has_next and p == 8:
                        at[0] = 0
                        prepare_shift(c + 1)
                    if has_next and p == 10:
                        prepare_sum(c + 1)
                    if has_next and p == 11:
                        prepare_top(c + 1)
                    if has_next and p == 12:
                        prepare_chosen(c + 1)
                    if has_next and p == 13:
                        prepare_part1(c + 1)
                    if p == 14:
                        zero_experts(c, par)
                    dve.wait_ge(gated_done, q + 1)
                    dve.wait_ge(route_mm, q + 1)
                    wait(dve, lo_done, q - 3)
                    v.tensor_tensor(act4[:, p % 4, :], gated[:, p % 2, :], bank[:, ROUTE_B[p % 2], :], ALU.mult).then_inc(act_done, 1)
                    if has_next and p == 10:
                        prepare_scores(c + 1)
                    if has_prev and p == 10:
                        finish(c - 1)
                    if has_next and p == 11:
                        prepare_mark(c + 1)
                    if has_next and p == 12:
                        prepare_weights(c + 1)
                    if has_next and p == 13:
                        prepare_part2(c + 1)
                        prepare_part3(c + 1)

            dve.wait_ge(res_done, B)
            dve.wait_ge(v_done, 1)
            v.tensor_tensor(h_all[:, 0, :, :], v_t[:, :, :], h_all[:, 0, :, :], ALU.add).then_inc(x1_done, 1)
            prepare_stats(0)
            prepare_moments(0)
            prepare_v(1)
            dve.wait_ge(rstd3_done, 1)
            for j in range(NT):
                done = v.tensor_scalar(z[:, j, :], h_all[:, 0, j, :], rs3[:, j:j + 1], mr3[:, j:j + 1], ALU.mult, ALU.add)
            done.then_inc(z_done, 1)
            dve.wait_ge(stats3_done, 1)
            prepare_stats(1)
            prepare_shift(0)
            prepare_sum(0)
            prepare_scores(0)
            prepare_top(0)
            prepare_mark(0)
            prepare_chosen(0)
            prepare_weights(0)
            prepare_part1(0)
            prepare_part2(0)
            prepare_part3(0)
            experts(0, 0, False, True, True)
            with dve.Fori(0, (B - 4) // 2) as i:
                experts(i * 2 + 1, 1, True, True, True)
                experts(i * 2 + 2, 0, True, True, True)
            experts(B - 3, 1, True, True, True)
            experts(B - 2, 0, True, True, False)
            experts(B - 1, 1, True, False, False)
            last = (PAIRS - 1) % 4
            dve.wait_ge(down_mm, B * PAIRS - 4)
            dve.wait_ge(hi_done, B * PAIRS)
            dve.wait_ge(lo_done, B * PAIRS - 1)
            v.tensor_tensor(act_lo[:, last, :], act4[:, last, :], act_hi[:, last, :].bitcast(F32),
                            ALU.subtract).then_inc(lo_done, 1)
            leave_down(B - 1, 1)
            finish(B - 1)

        @block.tensor
        def _(pe):
            mm = nc.tensor.matmul
            def keep_warm(to, times, cols=512):
                for _ in range(times):
                    mm(to[:, 512 - cols:512], zero_bf[:, :], zero_bf[:, :].unsqueeze(1).broadcast_to([P, cols // P, P]),
                       start=True, stop=True)

            pe.wait_ge(zero_made, 1)
            keep_warm(bank[:, PROJ_B[0], :], 7)
            pe.wait_ge(pool_const, N_SETUP_CONST)
            pe.wait_ge(c_silu_done, 1)
            nc.tensor.transpose(bank[:, SETUP_B, 0:B], c_silu[:, :], ident[0:B, 0:B]).then_inc(ct_mm, 1)
            keep_warm(bank[:, PROJ_B[0], :], 1)
            pe.wait_ge(ct_done, 1)
            pe.wait_ge(in_wmod, 16)

            def make_rows(k):
                _, vector, half = ROW_ORDER[k]
                for r in range(4):
                    b = 4 * half + r
                    left, right = ((modt[:, GA, b:b + 1], ident[:, 0:P]) if vector == GA
                                   else (c_silu_t[:, b:b + 1], wmod_sb[:, vector * P:(vector + 1) * P]))
                    done = mm(bank[:, ROWS_B[k], r * P:(r + 1) * P], left.broadcast_to([P, P]), right, start=True, stop=True)
                done.then_inc(rows_mm, 1)

            make_rows(0)
            make_rows(1)
            for m in range(GA, NMOD):
                done = mm(bank[:, SETUP_B, m * B:(m + 1) * B], wmod_sb[:, m * P:(m + 1) * P], c_silu_t[:, :], start=True, stop=True)
            done.then_inc(mod_mm, 1)
            make_rows(2)
            make_rows(3)
            pe.wait_ge(ga_done, 1)
            make_rows(4)
            make_rows(5)
            for g in range(GROUPS):
                mm(bank[:, SETUP_B, AT_GA + g * P:AT_GA + (g + 1) * P], ga_rep[:, g, :, :].rearrange("d b s -> d (b s)"), ident[:, 0:P],
                   start=True, stop=True)
            pe.wait_ge(in_small, 64)
            pe.wait_ge(in_late, 64)
            mm(bank[:, SETUP_B, AT_SMALL:AT_SMALL + S + P + 1], spread_rows[:, 0, :, :, :].rearrange("k b w s -> k (b w s)"),
               small[:, 0:S + P + 1], start=True, stop=True)
            mm(bank[:, SETUP_B, AT_SMALL + S + P:AT_SMALL + S + P + 1], spread_rows[:, 1, :, :, :].rearrange("k b w s -> k (b w s)"),
               small[:, S + P + 1:S + P + 2], start=False, stop=True, skip_group_check=True)
            nc.tensor.transpose(bank[:, SETUP_B, AT_CLS:AT_CLS + E_T], cls_sb[:, :], ident[0:E_T, 0:E_T]).then_inc(ga_rep_mm, 1)

            pe.wait_ge(rows_dve, 2)
            pe.wait_ge(rows_act, 4)
            pe.wait_ge(in_w, 32)

            def project(b):
                pe.wait_ge(xnt_done, b + 1)
                b4, g = b // GROUPS, b % GROUPS
                lo = W_PAD - 2 * S * b4
                done = mm(bank[:, PROJ_B[g], :], w_pad[:, lo:lo + P], xn_all[:, b, :], start=b4 == 0, stop=b4 == BG - 1)
                if b4 == BG - 1:
                    done.then_inc(proj_done, 1)

            for b in range(B):
                pe.wait_ge(z2_done, b + 1)
                wait(pe, xnt_done, b - 1)
                for j in range(NT):
                    done = nc.tensor.transpose(bank[:, MISC[b % 2], j * P:(j + 1) * P], xn_all[:, b, j * P:(j + 1) * P], ident[:, 0:P])
                done.then_inc(z2t_done, 1)
                if b:
                    project(b - 1)
                    if b < B - 3:
                        keep_warm(bank[:, ROWS_B[0], :], 4)
            project(B - 1)
            keep_warm(bank[:, ROWS_B[0], :], 4)
            def make_y(n, g):
                for j in range(NT):
                    done = mm(bank[:, PREP_B, j * P:(j + 1) * P], H[:, g * T + j * P:g * T + (j + 1) * P], c_batch[:, n, :], start=True, stop=True)
                return done

            def seed(dst, cols, last):
                return mm(dst, ident[:, S:S + P], drive[:, cols], start=True, stop=last)

            def side(n):
                kind, m = SIDE_WORK[n]
                to = bank[:, SIDE[n % NS], :]
                if n >= NS:
                    pe.wait_ge(*side_read(n - NS))
                if kind == "weights":
                    which, g = m // 4, m % 4
                    pe.wait_ge(in_dn if which == 2 else in_gu, 16 if which == 2 else 64)
                    for r in range(4):
                        pair = 4 * g + r
                        src = (dn_raw[:, 2 * pair:2 * pair + 2, :].rearrange("h e i -> h (e i)") if which == 2
                               else gu_raw[:, which, pair, :])
                        done = nc.tensor.transpose(to[:, r * P:(r + 1) * P], src, ident[:, 0:P])
                else:
                    b, half = m // 2, m % 2
                    mm(to[:, 0:256], ones3[:, :], bg_rows[:, :].unsqueeze(1).broadcast_to([3, 2, P]), start=True, stop=True)
                    for j in range(2):
                        j0 = (2 * half + j) * P
                        done = mm(to[:, j * P:(j + 1) * P], xn_all[:, b, j0:j0 + P], wg_sb[:, :],
                                  start=False, stop=True, skip_group_check=True)
                done.then_inc(side_mm, 1)

            pe.wait_ge(bg_done, 1)
            pe.wait_ge(drive_out, GROUPS)
            pe.wait_ge(delta_out, GROUPS)
            a_all = a_block[:, :, :, :].rearrange("p b w s -> p (b w s)")
            seed(bank[:, SCAN[0], 0:COLS], slice(0, None, SEG_LEN), True).then_inc(step_mm, 1)
            for n in range(1, SWEEP_STEPS):
                k = n % SEG_LEN
                dst = bank[:, SCAN[n % 2], 0:COLS]
                keep_warm(bank[:, SCAN[n % 2], :], 1 if n < len(SIDE_WORK) else 3, 256)
                seed(dst, slice(k, None, SEG_LEN), False)
                if n - 1 < len(SIDE_WORK):
                    side(n - 1)
                pe.wait_ge(step_in, n)
                mm(dst, a_all, (h_in if k else h_in0)[:, :], start=False, stop=True).then_inc(step_mm, 1)
            keep_warm(bank[:, SCAN[0], :], 7, 256)
            pe.wait_ge(step_in, SWEEP_STEPS)
            mm(bank[0:1, SCAN[0], 0:1], differ_p[:, :], ones_col[:, :], start=True, stop=True).then_inc(verdict_mm, 1)
            pe.wait_ge(side_lo, N_WEIGHTS)
            pe.wait_ge(side_gate, N_GATES)
            make_y(0, 0).then_inc(y_mm, 1)
            pe.wait_ge(verdict, 1)
            go_on = pe.value_load(again[0:1, 0:1])
            with pe.If(go_on != 0):
                with pe.Fori(0, SEGS - 2) as s:
                    with pe.Fori(0, SEG_LEN) as k:
                        pe.wait_ge(more_in, s * SEG_LEN + k + 1)
                        seed(bank[:, SCAN[0], 0:COLS], bass.ds(k, COLS, SEG_LEN), False)
                        mm(bank[:, SCAN[0], 0:COLS], a_all, h_in[:, :],
                           start=False, stop=True).then_inc(more_mm, 1)
                pe.wait_ge(more_h, (SEGS - 2) * SEG_LEN)
                pe.wait_ge(v_done, 1)
                make_y(0, 0).then_inc(more_y, 1)
                pe.wait_ge(more_v, 1)

            def prepare_y(n, g):
                if not isinstance(n, int) or n >= 2:
                    pe.wait_ge(weight_t_done, n - 1)
                elif n == 1:
                    pe.wait_ge(v_done, 1)
                make_y(n, g).then_inc(y_mm, 1)

            def prepare_zt(n, has_more):
                pe.wait_ge(z_done, n + 1)
                if has_more:
                    pe.wait_ge(v_done, n + 2)
                else:
                    pe.wait_ge(weight_t_done, n)
                for j in range(NT):
                    done = nc.tensor.transpose(bank[:, PREP_B, j * P:(j + 1) * P], z[:, j, :], ident[:, 0:P])
                done.then_inc(zt_mm, 1)

            def prepare_logits(n, par):
                pe.wait_ge(h2t_done, n + 1)
                for j in range(NT):
                    done = mm(bank[:, PREP_B, j * E_T:(j + 1) * E_T], h2t[par][:, j * P:(j + 1) * P], cls_t[:, :], start=True, stop=True)
                done.then_inc(logit_mm, 1)

            def prepare_weights(n):
                pe.wait_ge(weight_done, n + 1)
                wait(pe, zero_done, n)
                to = bank[0:W_ROWS, PREP_B, :].bitcast(BF16)
                for j in range(NT):
                    done = nc.tensor.transpose(to[:, j * P:(j + 1) * P], w3[:, j, :, :].rearrange("p k e -> p (k e)"), ident_bf[:, :])
                done.then_inc(weight_mm, 1)

            def zero_product(c):
                wait(pe, out_ready, c)
                mm(bank[:, PREP_B, :], pick_zero[:, :], w3t[:, :], start=True, stop=True).then_inc(zero_mm, 1)

            def split_product(dst, which, pair, hi, lo, first=True, last=True):
                mm(dst, w_hi[:, which, pair, :], hi, start=first, stop=False)
                mm(dst, w_hi[:, which, pair, :], lo, start=False, stop=False)
                return mm(dst, w_lo[:, which, pair, :], hi, start=False, stop=last)

            def route(c, p):
                wait(pe, act_done, c * PAIRS + p - 1)
                mm(bank[:, ROUTE_B[p % 2], :], pick_pair[:, p, :], w3t[:, :], start=True, stop=True).then_inc(route_mm, 1)

            LAG = 3

            def down_product(c, p):
                q = c * PAIRS + p
                if p == 0:
                    wait(pe, f_done, c)
                pe.wait_ge(lo_done, q + 1)
                pe.wait_ge(hi_done, q + 1)
                split_product(bank[:, DOWN_B, :], 2, p, act_hi[:, p % 4, :], act_lo[:, p % 4, :],
                              p == 0, p == PAIRS - 1).then_inc(down_mm, 1)

            def transpose_down(c, has_next):
                pe.wait_ge(f_done, c + 1)
                if has_next:
                    pe.wait_ge(shifted_done, c + 3)
                else:
                    pe.wait_ge(weight_t_done, B)
                    if c == B - 1:
                        pe.wait_ge(zero_done, B)
                for j in range(NT):
                    done = nc.tensor.transpose(bank[:, PREP_B, j * P:(j + 1) * P], f_t[:, j * P:(j + 1) * P], ident[:, 0:P])
                done.then_inc(ft_mm, 1)

            def gate_product(c, par, p):
                wait(pe, silu_done, c * PAIRS + p - 1)
                split_product(bank[:, GATE_B[p % 2], :], 0, p, h2_hi[:, par, :], h2_lo[:, par, :]).then_inc(gate_mm, 1)

            def experts(c, par, has_prev, has_next, has_two):
                for p in range(PAIRS):
                    q = c * PAIRS + p
                    if p == 0:
                        pe.wait_ge(h2_lo_done, c + 1)
                    if p != (1 if has_prev else 2):
                        gate_product(c, par, p)
                    wait(pe, gated_done, q - 1)
                    split_product(bank[:, UP_B[p % 2], :], 1, p, h2_hi[:, par, :], h2_lo[:, par, :]).then_inc(up_mm, 1)
                    if has_next and p == 7:
                        prepare_logits(c + 1, 1 - par)
                    if p == 1 and not has_prev:
                        gate_product(c, par, 2)
                        keep_warm(bank[:, ROUTE_B[0], :], 8)
                    if p == (0 if has_prev else 1):
                        prepare_weights(c)
                        if has_prev:
                            down_product(c - 1, PAIRS - LAG)
                            gate_product(c, par, 1)
                        pe.wait_ge(weight_t_done, c + 1)
                        if not has_prev:
                            route(c, 0)
                    if p or has_prev:
                        route(c, p)
                    if p == LAG + 1:
                        down_product(c, 0)
                    if p > LAG:
                        down_product(c, p - LAG)
                    elif has_prev and 0 < p < LAG:
                        down_product(c - 1, PAIRS - LAG + p)
                    if has_next and p == 4:
                        prepare_zt(c + 1, has_two)
                    if has_prev and p == 9:
                        transpose_down(c - 1, has_next)
                    if p == 12:
                        zero_product(c)
                    if has_two and p == 1:
                        prepare_y(c + 2, par)

            pe.wait_ge(pool_const, N_POOL_CONST)
            keep_warm(bank[:, UP_B[0], :], 3)
            prepare_y(1, 1)
            keep_warm(bank[:, UP_B[0], :], 12)
            prepare_zt(0, True)
            keep_warm(bank[:, UP_B[0], :], 4)
            prepare_logits(0, 0)
            keep_warm(bank[:, UP_B[0], :], 4)
            experts(0, 0, False, True, True)
            with pe.Fori(0, (B - 4) // 2) as i:
                experts(i * 2 + 1, 1, True, True, True)
                experts(i * 2 + 2, 0, True, True, True)
            experts(B - 3, 1, True, True, True)
            experts(B - 2, 0, True, True, False)
            experts(B - 1, 1, True, False, False)
            for p in range(PAIRS - LAG, PAIRS):
                down_product(B - 1, p)
            transpose_down(B - 1, False)


_INS = ['L0_attn_x', 'L0_attn_ln_gamma', 'L0_attn_ln_beta', 'L0_attn_A', 'L0_attn_C', 'L0_attn_w_delta',
        'L0_attn_b_delta', 'L0_attn_w_in', 'L0_attn_b_in', 'L0_attn_w_gate', 'L0_attn_b_gate',
        'L0_ffn_classifier_weight', 'L0_ffn_e_score_correction_bias', 'L0_ffn_gate_up_proj', 'L0_ffn_down_proj',
        'L0_c', 'L0_wmod']


def kernel(**inputs):
    import numpy as _np
    import concourse.bacc as _bacc
    from concourse import mybir as _mybir
    from concourse.bass_utils import run_bass_kernel_spmd as _run

    nc = _bacc.Bacc("TRN2", target_bir_lowering=False, num_devices=1)
    arrays, args = {}, []
    for name in _INS:
        a = _np.ascontiguousarray(inputs[name])
        arrays[f"in_{name}_dram"] = a
        args.append(nc.dram_tensor(f"in_{name}_dram", a.shape, _mybir.dt.from_np(a.dtype), kind="ExternalInput").ap())
    shape = inputs['L0_attn_x'].shape
    args.append(nc.dram_tensor("out_0_dram", shape, F32, kind="ExternalOutput").ap())
    adaln_block(nc, *args)
    r = _run(nc, [arrays], core_ids=[0])
    return r.results[0]["out_0_dram"]
```
